# Optimizing a Trainium2 kernel written in Bass

```python
import numpy as np
import jax
import jax.numpy as jnp

def _softmax(x, axis=-1):
    return jax.nn.softmax(x, axis=axis)

def _gelu(x):
    return jax.nn.gelu(x, approximate=True)

def _silu(x):
    return jax.nn.silu(x)

def _sigmoid(x):
    return jax.nn.sigmoid(x)

def _layernorm(x, axis=-1, eps=1e-05):
    m = jnp.mean(x, axis=axis, keepdims=True)
    v = jnp.var(x, axis=axis, keepdims=True)
    return (x - m) / jnp.sqrt(v + eps)

def _scatter_add(tgt, idx, src, axis=0):
    return tgt.at[idx].add(src)

def _segment_sum(src, seg, n):
    return jax.ops.segment_sum(src, seg, n)
kernel_name = 'mk_adj_ffn_d1_adj_r2_b35186'

def setup_inputs(seed: int=0):
    np.random.seed(seed)
    _w = jnp.asarray

    def _rec_inputs():
        import jax
        import jax.numpy as jnp
        _gk = jax.random.key(seed)
        x = -8.776e-05 + 1 * jax.random.normal(jax.random.fold_in(_gk, 1), (10000, 128), jnp.float32)
        _w = (1.0 + jnp.arange(10000, dtype=jnp.float32)) ** (-0.5)
        _w = _w / _w.mean()
        _pij = jnp.clip(0.0002 * _w[:, None] * _w[None, :], 0.0, 1.0)
        _a = jax.random.uniform(jax.random.fold_in(_gk, 2), (10000, 10000)) < _pij
        _a = jnp.logical_or(_a, jnp.eye(10000, dtype=bool))
        _af = _a.astype(jnp.float32)
        _af = _af * jax.random.uniform(jax.random.fold_in(_gk, 3), (10000, 10000), jnp.float32, 0.05, 1)
        adj = _af
        return (x, adj)
    x, adj = _rec_inputs()

    def _L0_gnn_setup():
        import jax, jax.numpy as jnp
        import numpy as np
        N_USER = 10000
        N_ITEM = 10000
        HID = 128
        key = jax.random.key(seed)
        k1, k2, k3, k4, k5, k6, k7 = jax.random.split(key, 7)
        scale = 1.0 / np.sqrt(HID)
        return {'user_feat': jax.random.normal(k1, (N_USER, HID), dtype=jnp.float32), 'item_feat': jax.random.normal(k2, (N_ITEM, HID), dtype=jnp.float32), 'adj': jax.random.uniform(k3, (N_USER, N_ITEM), dtype=jnp.float32), 'W_item': jax.random.uniform(k4, (HID, HID), dtype=jnp.float32, minval=-scale, maxval=scale), 'b_item': jax.random.uniform(k5, (HID,), dtype=jnp.float32, minval=-scale, maxval=scale), 'W_user': jax.random.uniform(k6, (HID, HID), dtype=jnp.float32, minval=-scale, maxval=scale), 'b_user': jax.random.uniform(k7, (HID,), dtype=jnp.float32, minval=-scale, maxval=scale)}
    _L0_gnn_all = _L0_gnn_setup()
    _L0_gnn_in = {k: v for k, v in _L0_gnn_all.items() if k in ('item_feat', 'W_item', 'b_item', 'W_user', 'b_user')}
    del _L0_gnn_all

    def _L0_ffn_setup():
        import jax, jax.numpy as jnp
        import numpy as np
        D_MODEL = 128
        EXPERT_DIM = 256
        NUM_EXPERTS = 8
        TOP_K = 2
        SEQ_LEN = 1024
        BATCH = 2
        key = jax.random.key(seed)
        ks = jax.random.split(key, 8)
        s = 0.02
        x = jax.random.normal(ks[0], (SEQ_LEN, BATCH, D_MODEL), dtype=jnp.float32)
        Wg = jax.random.normal(ks[1], (D_MODEL, NUM_EXPERTS), dtype=jnp.float32) * s
        bg = jax.random.normal(ks[2], (NUM_EXPERTS,), dtype=jnp.float32) * s
        bias = jnp.zeros((NUM_EXPERTS,), dtype=jnp.float32)
        W1 = jax.random.normal(ks[3], (NUM_EXPERTS, D_MODEL, EXPERT_DIM), dtype=jnp.float32) * s
        b1 = jax.random.normal(ks[4], (NUM_EXPERTS, EXPERT_DIM), dtype=jnp.float32) * s
        W2 = jax.random.normal(ks[5], (NUM_EXPERTS, EXPERT_DIM, D_MODEL), dtype=jnp.float32) * s
        b2 = jax.random.normal(ks[6], (NUM_EXPERTS, D_MODEL), dtype=jnp.float32) * s
        return {'x': x, 'Wg': Wg, 'bg': bg, 'bias': bias, 'W1': W1, 'b1': b1, 'W2': W2, 'b2': b2}
    _L0_ffn_all = _L0_ffn_setup()
    _L0_ffn_in = {k: v for k, v in _L0_ffn_all.items() if k in ('Wg', 'bg', 'bias', 'W1', 'b1', 'W2', 'b2')}
    del _L0_ffn_all
    return {'x': x, 'adj': adj, 'L0_gnn_item_feat': _L0_gnn_in['item_feat'], 'L0_gnn_W_item': _L0_gnn_in['W_item'], 'L0_gnn_b_item': _L0_gnn_in['b_item'], 'L0_gnn_W_user': _L0_gnn_in['W_user'], 'L0_gnn_b_user': _L0_gnn_in['b_user'], 'L0_ffn_Wg': _L0_ffn_in['Wg'], 'L0_ffn_bg': _L0_ffn_in['bg'], 'L0_ffn_bias': _L0_ffn_in['bias'], 'L0_ffn_W1': _L0_ffn_in['W1'], 'L0_ffn_b1': _L0_ffn_in['b1'], 'L0_ffn_W2': _L0_ffn_in['W2'], 'L0_ffn_b2': _L0_ffn_in['b2']}

def reference(x, adj, L0_gnn_item_feat, L0_gnn_W_item, L0_gnn_b_item, L0_gnn_W_user, L0_gnn_b_user, L0_ffn_Wg, L0_ffn_bg, L0_ffn_bias, L0_ffn_W1, L0_ffn_b1, L0_ffn_W2, L0_ffn_b2):
    import jax
    import jax.numpy as jnp

    def _L0_gnn_ref(user_feat, item_feat, adj, W_item, b_item, W_user, b_user):
        import jax, jax.numpy as jnp
        import numpy as np
        N_USER = 10000
        N_ITEM = 10000
        HID = 128
        h = item_feat @ W_item.T + b_item
        b = user_feat @ W_user.T + b_user
        return jax.nn.relu(adj @ h + b)

    def _L0_ffn_ref(x, Wg, bg, bias, W1, b1, W2, b2):
        import jax, jax.numpy as jnp
        import numpy as np
        D_MODEL = 128
        EXPERT_DIM = 256
        NUM_EXPERTS = 8
        TOP_K = 2
        SEQ_LEN = 1024
        BATCH = 2
        x_flat = x.reshape(-1, D_MODEL)
        gate_logits = x_flat @ Wg + bg + bias
        topk_vals, topk_idx = jax.lax.top_k(gate_logits, TOP_K)
        topk_w = jax.nn.softmax(topk_vals, axis=-1)
        combine = (jax.nn.one_hot(topk_idx, NUM_EXPERTS, dtype=x.dtype) * topk_w[..., None]).sum(axis=1)
        h = jax.nn.relu(jnp.einsum('td,edh->teh', x_flat, W1) + b1)
        y = jnp.einsum('teh,ehd->ted', h, W2) + b2
        out = jnp.einsum('ted,te->td', y, combine)
        return out.reshape(x.shape)
    x = x + _L0_gnn_ref(_layernorm(x, axis=-1), L0_gnn_item_feat, adj, L0_gnn_W_item, L0_gnn_b_item, L0_gnn_W_user, L0_gnn_b_user)
    x = x + _L0_ffn_ref(_layernorm(x, axis=-1)[None], L0_ffn_Wg, L0_ffn_bg, L0_ffn_bias, L0_ffn_W1, L0_ffn_b1, L0_ffn_W2, L0_ffn_b2)[0]
    return x

_drawn_inputs = setup_inputs


def setup_inputs(seed=0):
    import zlib

    import numpy as np

    out = dict(_drawn_inputs(seed))
    spreads = {'L0_ffn_bias': (0.0, 0.319)}
    factors = {'L0_ffn_bg': 23.505, 'L0_ffn_b1': 23.149, 'L0_ffn_b2': 4.498}
    for name, (base, spread) in spreads.items():
        noise = np.random.default_rng([zlib.crc32(name.encode()), seed]).standard_normal(out[name].shape)
        drawn = base * np.exp(spread * noise) if base else spread * noise
        out[name] = jnp.asarray(drawn.astype(out[name].dtype))
    for name, factor in factors.items():
        out[name] = (out[name] * factor).astype(out[name].dtype)
    return out
```

```python
from contextlib import ExitStack

import concourse.bass as bass
from concourse import mybir

F32 = mybir.dt.float32
F32R = mybir.dt.float32r
U32 = mybir.dt.uint32
ALU = mybir.AluOpType
ACT = mybir.ActivationFunctionType

P = 128
N = 10000
D = 128
E = 8
H = 256
HC = E * H // P
BLOCK = 500
BLOCKS = N // BLOCK
Q = 4
QU = BLOCK // Q
TILES = -(-N // P)
CHUNKS = [4] * 16 + [3] * 5
CH = len(CHUNKS)
FIRST = [sum(CHUNKS[:c]) for c in range(CH + 1)]
RING = 3
assert sum(CHUNKS) == TILES and CH % RING == 0
ITEM_TILES = 10
ITEM_LOADS = -(-TILES // ITEM_TILES)
GROUPS = -(-TILES // 4)
WEIGHT_LOADS = 4
HALF = HC * P // 2
RAW0 = ITEM_LOADS + WEIGHT_LOADS
assert RAW0 % RING == 0
HR = 3
HB = 3
EPS = 1e-5

TURN_X1, TURN_LN, GATE, TURN_C, EXPERTS, TURN_X = 6, 11, 14, 24, 26, 60
USER = 74
LAYER1 = [EXPERTS + round(2.8 * k) for k in range(HC)]
LAG = 3

C_ID, C_WU, C_WG, C_B1, C_BU, C_IOTA, C_END = 0, 128, 256, 264, 280, 281, 313
S_WI, S_B2, S_BG, S_BIAS, S_END = 0, 128, 256, 288, 320


def chunk_of(slot):
    return next(c for c in range(CH) if slot < FIRST[c + 1])


def build(nc, adjT, itemT, x, xT, w1, w2, consts, item_bias, selectors, start, outT):
    with ExitStack() as ctx:
        def sb(name, shape, dt=F32):
            return ctx.enter_context(nc.sbuf_tensor(name, shape, dt))

        def ps(name, shape):
            return ctx.enter_context(nc.psum_tensor(name, shape, F32))

        def sem(name):
            return ctx.enter_context(nc.semaphore(name))

        raw = sb("raw", [P, RING, 4 * BLOCK])
        adj_hi = sb("adj_hi", [P, RING, 4 * BLOCK], F32R)
        adj_lo = sb("adj_lo", [P, RING, 4 * BLOCK], F32R)
        h_hi = sb("h_hi", [P, TILES, D], F32R)
        h_lo = sb("h_lo", [P, TILES, D], F32R)
        w1_hi = sb("w1_hi", [P, HC * P], F32R)
        w1_lo = sb("w1_lo", [P, HC * P], F32R)
        w2_hi = sb("w2_hi", [P, HC * P], F32R)
        w2_lo = sb("w2_lo", [P, HC * P], F32R)
        cst = sb("cst", [P, C_END])
        gate_bias = sb("gate_bias", [QU, Q, E])
        select = sb("select", [2 * E, E, P], F32R)
        b2_hi = sb("b2_hi", [2 * E, D], F32R)
        b2_lo = sb("b2_lo", [2 * E, D], F32R)
        rows = sb("rows", [P, Q * D])
        cols = sb("cols", [P, BLOCK])
        xT_sb = sb("xT_sb", [P, BLOCK])
        x1T = sb("x1T", [P, BLOCK])
        ln_hi = sb("ln_hi", [P, BLOCK], F32R)
        ln_lo = sb("ln_lo", [P, BLOCK], F32R)
        pre = sb("pre", [P, 2, Q * D])
        hid_hi = sb("hid_hi", [P, HR, BLOCK], F32R)
        hid_lo = sb("hid_lo", [P, HR, BLOCK], F32R)
        wgt_sb = sb("wgt_sb", [P, 2, BLOCK])
        stats = sb("stats", [QU, 2, Q, 6])
        moments = sb("moments", [QU, 2, Q, 2])
        var_eps = sb("var_eps", [QU, 2, Q])
        rstd = sb("rstd", [QU, 2, Q])
        spacer = sb("spacer", [1, 1])
        minus_half = sb("minus_half", [QU, Q])
        logits = sb("logits", [QU, Q, E])
        top = sb("top", [QU, Q, 8])
        top_at = sb("top_at", [QU, Q, 8], U32)
        top_f = sb("top_f", [QU, Q, 2])
        gap = sb("gap", [QU, Q])
        egap = sb("egap", [QU, Q])
        den = sb("den", [QU, Q])
        wt = sb("wt", [QU, 2, Q])
        hot = sb("hot", [QU, 2, Q, E])
        comb = sb("comb", [QU, Q, E])
        comb_hi = sb("comb_hi", [QU, Q, E], F32R)
        comb_two = sb("comb_two", [QU, Q, 2 * E])
        combT = sb("combT", [2 * E, BLOCK], F32R)

        ident = cst[:, C_ID:C_ID + P]
        wiT = xT_sb[:, S_WI:S_WI + D]
        b2_raw = xT_sb[0:2 * E, S_B2:S_B2 + D]
        wuT = cst[:, C_WU:C_WU + D]
        wg = cst[:, C_WG:C_WG + E]
        b1 = cst[:, C_B1:C_B1 + HC]
        b_user = cst[:, C_BU:C_BU + 1]
        iota = cst[0:QU, C_IOTA:C_IOTA + Q * E].rearrange("p (q e) -> p q e", q=Q)
        bg = xT_sb[0:QU, S_BG:S_BG + Q * E].rearrange("p (q e) -> p q e", q=Q)
        bias = xT_sb[0:QU, S_BIAS:S_BIAS + Q * E].rearrange("p (q e) -> p q e", q=Q)
        rows3 = rows[0:QU, :].rearrange("p (q d) -> p q d", q=Q)

        acc = ps("acc", [P, 512])
        y = ps("y", [P, 512])
        hid = [ps(f"hid{i}", [P, 512]) for i in range(HB)]
        wgt = ps("wgt", [P, 512])
        turn_a = ps("turn_a", [P, 512])
        turn_b = ps("turn_b", [P, 512])

        const_loaded = sem("const_loaded")
        raw_loaded = [sem(f"raw_loaded{i}") for i in range(RING)]
        item_used = sem("item_used")
        h_made = sem("h_made")
        h_full = sem("h_full")
        h_hi_made = sem("h_hi_made")
        h_lo_made = sem("h_lo_made")
        w_hi_made = sem("w_hi_made")
        w_lo_made = sem("w_lo_made")
        half_made = sem("half_made")
        small_made = sem("small_made")
        hi_ready = sem("hi_ready")
        lo_ready = sem("lo_ready")
        chunk_used = sem("chunk_used")
        acc_done = sem("acc_done")
        acc_read = sem("acc_read")
        x_loaded = sem("x_loaded")
        xT_loaded = sem("xT_loaded")
        x_stats = sem("x_stats")
        x_rstd = sem("x_rstd")
        x_normed = sem("x_normed")
        x_turned = sem("x_turned")
        xcols_ready = sem("xcols_ready")
        x1_ready = sem("x1_ready")
        x1_turned = sem("x1_turned")
        x1_stats = sem("x1_stats")
        x1_rstd = sem("x1_rstd")
        x1_normed = sem("x1_normed")
        ln_turned = sem("ln_turned")
        ln_cols = sem("ln_cols")
        ln_hi_made = sem("ln_hi_made")
        ln_lo_made = sem("ln_lo_made")
        gate_done = sem("gate_done")
        router = sem("router")
        gap_ready = sem("gap_ready")
        egap_ready = sem("egap_ready")
        comb_ready = sem("comb_ready")
        comb_turned = sem("comb_turned")
        combT_ready = sem("combT_ready")
        wgt_done = sem("wgt_done")
        wgt_copied = sem("wgt_copied")
        hid_done = sem("hid_done")
        pre_ready = sem("pre_ready")
        hid_hi_made = sem("hid_hi_made")
        hid_lo_made = sem("hid_lo_made")
        hid_used = sem("hid_used")
        y_done = sem("y_done")
        out_ready = sem("out_ready")
        out_stored = sem("out_stored")
        ROUTER_STEPS = 10
        SMALL = 4

        block = ctx.enter_context(nc.Block())

        @block.sync
        def _(sp):
            sp.dma_start(cst[:, :], consts).then_inc(const_loaded, 16)
            sp.dma_start(rows[:, :], item_bias).then_inc(const_loaded, 16)
            sp.dma_start(pre[0:2 * E, :, :].rearrange("p a b -> p (a b)"), selectors).then_inc(const_loaded, 16)
            sp.dma_start(xT_sb[:, 0:S_END], start).then_inc(const_loaded, 16)

            def load_start(m):
                if m >= RING:
                    if m - RING < ITEM_LOADS:
                        sp.wait_ge(item_used, m - RING + 1)
                    else:
                        sp.wait_ge(w_lo_made, m - RING - ITEM_LOADS + 1)
                if m < ITEM_LOADS:
                    t0, t1 = m * ITEM_TILES, min((m + 1) * ITEM_TILES, TILES)
                    src = itemT[:, t0 * P:t1 * P]
                else:
                    i = m - ITEM_LOADS
                    src = (w1 if i < 2 else w2)[:, (i % 2) * HALF:(i % 2 + 1) * HALF]
                sp.dma_start(raw[:, m % RING, 0:src.shape[1]], src).then_inc(raw_loaded[m % RING], 16)

            def load_adj(b, c):
                src = adjT[bass.ds(b, 1), :, FIRST[c] * BLOCK:FIRST[c + 1] * BLOCK].rearrange("a p n -> (a p) n")
                sp.dma_start(raw[:, c % RING, 0:CHUNKS[c] * BLOCK], src).then_inc(raw_loaded[c % RING], 16)

            def iteration(b, adj, next_adj, store):
                for c in range(CH):
                    if c + RING < CH and adj:
                        sp.wait_ge(lo_ready, b * CH + (c + 1))
                        load_adj(b, c + RING)
                    elif c + RING >= CH and next_adj:
                        sp.wait_ge(lo_ready, b * CH + (c + 1))
                        load_adj(b + 1, c + RING - CH)
                    if c == 1 and store:
                        sp.wait_ge(out_ready, b - 1)
                        sp.dma_start(outT[bass.ds(b - 2, 1), :, :].rearrange("a p n -> (a p) n"),
                                     rows[:, 0:BLOCK]).then_inc(out_stored, 16)
                    if c == 8 and adj:
                        if isinstance(b, int) and b == 0:
                            sp.wait_ge(h_full, GROUPS)
                        else:
                            sp.wait_ge(ln_turned, b)
                            sp.wait_ge(x1_ready, b)
                        sp.dma_start(rows3, x[bass.ds(b, 1), :, :].rearrange("a p (q d) -> (a p) q d", q=Q))\
                          .then_inc(x_loaded, 16)
                        sp.dma_start(xT_sb[:, :], xT[bass.ds(b, 1), :, :].rearrange("a p n -> (a p) n"))\
                          .then_inc(xT_loaded, 16)

            for m in range(RAW0):
                load_start(m)
            for c in range(RING):
                sp.wait_ge(w_lo_made, c + 2)
                load_adj(0, c)
            iteration(0, True, True, False)
            iteration(1, True, True, False)
            with sp.Fori(2, BLOCKS - 1) as b:
                iteration(b, True, True, True)
            iteration(BLOCKS - 1, True, False, True)
            iteration(BLOCKS, False, False, True)
            sp.wait_ge(out_ready, BLOCKS)
            sp.dma_start(outT[BLOCKS - 1], rows[:, 0:BLOCK]).then_inc(out_stored, 16)
            sp.wait_ge(out_stored, 16 * BLOCKS)

        @block.tensor
        def _(pe):
            def product(out, hi, lo, m_hi, m_lo, start, stop):
                pe.matmul(out, hi, m_hi, start=start, stop=False)
                pe.matmul(out, hi, m_lo, start=False, stop=False)
                return pe.matmul(out, lo, m_hi, start=False, stop=stop)

            def make_h():
                pe.wait_ge(const_loaded, 64)
                for g in range(GROUPS):
                    if g >= 2:
                        pe.wait_ge(h_full, g - 1)
                    for t in range(4 * g, min(4 * g + 4, TILES)):
                        m, i = divmod(t, ITEM_TILES)
                        if i == 0:
                            pe.wait_ge(raw_loaded[m % RING], 16 * (m // RING + 1))
                        mm = pe.matmul(hid[g % 2][:, (t % 4) * D:(t % 4 + 1) * D],
                                       raw[:, m % RING, i * P:(i + 1) * P], wiT, start=True, stop=True)
                        if i == ITEM_TILES - 1 or t == TILES - 1:
                            mm.then_inc(item_used, 1)
                            if t % 4 == 3 or t == TILES - 1:
                                pe.drain().then_inc(h_made, 1)
                        elif t % 4 == 3:
                            mm.then_inc(h_made, 1)

            def turn(out, source, rows_in, cols_in, done):
                for q in range(Q):
                    mm = pe.transpose(out(q), source(q), ident[0:rows_in, 0:rows_in])
                mm.then_inc(done, 1)

            def adj_tile(b, t):
                c = chunk_of(t)
                i = t - FIRST[c]
                if i == 0:
                    pe.wait_ge(hi_ready, b * CH + (c + 1))
                    pe.wait_ge(lo_ready, b * CH + (c + 1))
                at = slice(i * BLOCK, (i + 1) * BLOCK)
                mm = product(acc[:, 0:BLOCK], h_hi[:, t, :], h_lo[:, t, :],
                             adj_hi[:, c % RING, at], adj_lo[:, c % RING, at],
                             start=(t == 0), stop=(t == TILES - 1))
                if i == CHUNKS[c] - 1:
                    mm.then_inc(chunk_used, 1)

            def layer1(b, k):
                if k == 0:
                    pe.wait_ge(ln_hi_made, b)
                    pe.wait_ge(ln_lo_made, b)
                if k >= HB:
                    pe.wait_ge(pre_ready, b * HC + (k - HB + 1 - HC))
                at = slice(k * P, (k + 1) * P)
                product(hid[k % HB][:, 0:BLOCK], w1_hi[:, at], w1_lo[:, at], ln_hi[:, :], ln_lo[:, :],
                        start=True, stop=True).then_inc(hid_done, 1)

            def spread_weights(b, e):
                if e == 0:
                    pe.wait_ge(combT_ready, b)
                if e >= 1:
                    pe.wait_ge(wgt_copied, b * E + (e - E))
                pe.matmul(wgt[:, 0:BLOCK], select[:, e, :], combT[:, :],
                          start=True, stop=True).then_inc(wgt_done, 1)

            def layer2(b, k):
                pe.wait_ge(hid_hi_made, b * HC + (k + 1 - HC))
                pe.wait_ge(hid_lo_made, b * HC + (k + 1 - HC))
                at = slice(k * P, (k + 1) * P)
                product(y[:, 0:BLOCK], w2_hi[:, at], w2_lo[:, at], hid_hi[:, k % HR, :], hid_lo[:, k % HR, :],
                        start=(k == 0), stop=False).then_inc(hid_used, 1)

            def iteration(b, adj, prev):
                for s in range(TILES):
                    if adj:
                        if s == 0 and prev:
                            pe.wait_ge(acc_read, b)
                        adj_tile(b, s)
                    if prev and s == TURN_X1:
                        pe.wait_ge(x1_ready, b)
                        turn(lambda q: turn_a[0:QU, q * D:(q + 1) * D],
                             lambda q: x1T[:, q * QU:(q + 1) * QU], P, QU, x1_turned)
                    if prev and s == TURN_LN:
                        pe.wait_ge(x1_normed, b)
                        turn(lambda q: turn_b[:, q * QU:(q + 1) * QU], lambda q: rows3[:, q, :], QU, D, ln_turned)
                    if prev and s == GATE:
                        pe.wait_ge(ln_cols, b)
                        for q in range(Q):
                            mm = pe.matmul(turn_a[0:QU, q * E:(q + 1) * E], cols[:, q * QU:(q + 1) * QU], wg,
                                           start=True, stop=True)
                        mm.then_inc(gate_done, 1)
                    if prev and s == TURN_C:
                        pe.wait_ge(comb_ready, b)
                        pe.wait_ge(ln_lo_made, b)
                        turn(lambda q: turn_b[0:2 * E, q * QU:(q + 1) * QU],
                             lambda q: comb_two[:, q, :], QU, 2 * E, comb_turned)
                    for k in range(HC):
                        if prev and s == LAYER1[k]:
                            if k % 2 == 0:
                                spread_weights(b, k // 2)
                            layer1(b, k)
                            if k >= LAG:
                                layer2(b, k - LAG)
                    if adj and s == TURN_X:
                        pe.wait_ge(x_normed, b + 1)
                        turn(lambda q: turn_a[:, q * QU:(q + 1) * QU], lambda q: rows3[:, q, :], QU, D, x_turned)
                    if adj and s == USER:
                        pe.wait_ge(xcols_ready, b + 1)
                        pe.matmul(acc[:, 0:BLOCK], wuT, cols[:, :], start=False, stop=False)
                if adj:
                    pe.drain().then_inc(acc_done, 1)
                if prev:
                    for k in range(HC - LAG, HC):
                        layer2(b, k)
                    pe.matmul(y[:, 0:BLOCK], b2_hi[:, :], combT[:, :], start=False, stop=False)
                    pe.matmul(y[:, 0:BLOCK], b2_lo[:, :], combT[:, :], start=False, stop=True).then_inc(y_done, 1)

            make_h()
            pe.wait_ge(h_hi_made, GROUPS)
            pe.wait_ge(h_lo_made, GROUPS)
            pe.wait_ge(w_hi_made, WEIGHT_LOADS)
            pe.wait_ge(w_lo_made, WEIGHT_LOADS)
            pe.wait_ge(small_made, SMALL)
            iteration(0, True, False)
            with pe.Fori(1, BLOCKS) as b:
                iteration(b, True, True)
            iteration(BLOCKS, False, True)

        @block.scalar
        def _(act):
            def copy(out, in_):
                return act.activation(out, in_, ACT.Copy)

            def hi(b, c):
                act.wait_ge(raw_loaded[c % RING], b * (16 * CH // RING) + 16 * ((RAW0 + c) // RING + 1))
                if not (isinstance(b, int) and b == 0 and c < RING):
                    act.wait_ge(chunk_used, b * CH + (c - RING + 1))
                n = CHUNKS[c] * BLOCK
                copy(adj_hi[:, c % RING, 0:n], raw[:, c % RING, 0:n]).then_inc(hi_ready, 1)

            def copy_weights(b, e):
                act.wait_ge(wgt_done, b * E + (e + 1 - E))
                if e >= 2:
                    act.wait_ge(pre_ready, b * HC + (2 * (e - 1) - HC))
                copy(wgt_sb[:, e % 2, :], wgt[:, 0:BLOCK]).then_inc(wgt_copied, 1)

            def relu_hidden(b, k):
                act.wait_ge(pre_ready, b * HC + (k + 1 - HC))
                if k >= HR:
                    act.wait_ge(hid_used, b * HC + (k - HR + 1 - HC))
                act.activation(hid_hi[:, k % HR, :], pre[:, k % 2, 0:BLOCK], ACT.Relu).then_inc(hid_hi_made, 1)

            def iteration(b, adj, prev, next_adj):
                for c in range(CH):
                    if adj and c + 2 < CH:
                        hi(b, c + 2)
                    elif next_adj and c + 2 == CH:
                        hi(b + 1, 0)
                    if prev and c == chunk_of(TURN_LN):
                        act.wait_ge(ln_turned, b)
                        copy(cols[:, :], turn_b[:, 0:BLOCK]).then_inc(ln_cols, 1)
                        copy(ln_hi[:, :], turn_b[:, 0:BLOCK]).then_inc(ln_hi_made, 1)
                    if prev and c == chunk_of(TURN_C) - 1:
                        act.wait_ge(gap_ready, b)
                        act.activation(egap[:, :], gap[:, :], ACT.Exp).then_inc(egap_ready, 1)
                    if prev and c == chunk_of(TURN_C):
                        act.wait_ge(comb_turned, b)
                        copy(combT[:, :], turn_b[0:2 * E, 0:BLOCK]).then_inc(combT_ready, 1)
                    if prev:
                        for k in range(HC):
                            if chunk_of(LAYER1[k]) == c:
                                if k % 2 == 0:
                                    copy_weights(b, k // 2)
                                relu_hidden(b, k)
                    if adj and c == chunk_of(TURN_X):
                        act.wait_ge(x_turned, b + 1)
                        copy(cols[:, :], turn_a[:, 0:BLOCK]).then_inc(xcols_ready, 1)
                if adj:
                    act.wait_ge(acc_done, b + 1)
                    act.activation(cols[:, :], acc[:, 0:BLOCK], ACT.Relu, bias=b_user).then_inc(acc_read, 1)
                if next_adj:
                    hi(b + 1, 1)

            act.wait_ge(const_loaded, 64)
            copy(select[:, :, :].rearrange("p e m -> p (e m)"),
                 pre[0:2 * E, :, :].rearrange("p a b -> p (a b)")).then_inc(small_made, 1)
            copy(b2_hi[:, :], b2_raw).then_inc(small_made, 1)
            for g in range(GROUPS):
                n = min(4, TILES - 4 * g)
                act.wait_ge(h_full, g + 1)
                copy(h_hi[:, 4 * g:4 * g + n, :].rearrange("p t d -> p (t d)"),
                     pre[:, g % 2, 0:n * D]).then_inc(h_hi_made, 1)
            for i in range(WEIGHT_LOADS):
                m = ITEM_LOADS + i
                act.wait_ge(raw_loaded[m % RING], 16 * (m // RING + 1))
                copy((w1_hi if i < 2 else w2_hi)[:, (i % 2) * HALF:(i % 2 + 1) * HALF],
                     raw[:, m % RING, 0:HALF]).then_inc(w_hi_made, 1)
            hi(0, 0)
            hi(0, 1)
            iteration(0, True, False, True)
            with act.Fori(1, BLOCKS - 1) as b:
                iteration(b, True, True, True)
            iteration(BLOCKS - 1, True, True, False)
            iteration(BLOCKS, False, True, False)


        @block.gpsimd
        def _(pool):
            def root(i, steps, n, rooted):
                pool.wait_ge(steps, n * 3 + 3)
                pool.tensor_tensor(rstd[:, i, :], var_eps[:, i, :], minus_half[:, :], ALU.pow).then_inc(rooted, 1)

            pool.memset(minus_half[:, :], -0.5).then_inc(half_made, 1)
            pool.wait_ge(half_made, 1)
            root(1, x_stats, 0, x_rstd)
            with pool.Fori(1, BLOCKS) as b:
                root(0, x1_stats, b - 1, x1_rstd)
                root(1, x_stats, b, x_rstd)
            root(0, x1_stats, BLOCKS - 1, x1_rstd)

        @block.vector
        def _(dve):
            def lo(b, c):
                dve.wait_ge(hi_ready, b * CH + (c + 1))
                n = CHUNKS[c] * BLOCK
                dve.tensor_tensor(adj_lo[:, c % RING, 0:n], raw[:, c % RING, 0:n],
                                  adj_hi[:, c % RING, 0:n], ALU.subtract).then_inc(lo_ready, 1)

            def carry_wait():
                dve.memset(spacer[:, :], 0.0)

            def layernorm(source, i, n, steps, rooted, done):
                for q in range(Q):
                    last = dve.bn_stats(stats[:, i, q, :], source(q))
                last.then_inc(steps, 1)
                dve.wait_ge(steps, n * 3 + 1)
                carry_wait()
                for q in range(Q):
                    last = dve.bn_aggr(moments[:, i, q, :], stats[:, i, q, :])
                last.then_inc(steps, 1)
                dve.wait_ge(steps, n * 3 + 2)
                dve.tensor_scalar(var_eps[:, i, :], moments[:, i, :, 1], EPS, None, ALU.add).then_inc(steps, 1)
                dve.wait_ge(rooted, n + 1)
                for q in range(Q):
                    last = dve.tensor_scalar(rows3[:, q, :], source(q), moments[:, i, q, 0:1],
                                             rstd[:, i, q:q + 1], ALU.subtract, ALU.mult)
                last.then_inc(done, 1)

            def route(b):
                step = [0]

                def then(instruction):
                    step[0] += 1
                    instruction.then_inc(router, 1)
                    dve.wait_ge(router, b * ROUTER_STEPS + (step[0] - ROUTER_STEPS))

                def wide(v):
                    return v.broadcast_to([QU, Q, E])

                dve.wait_ge(gate_done, b)
                then(dve.tensor_tensor(logits[:, :, :], turn_a[0:QU, 0:Q * E].rearrange("p (q e) -> p q e", q=Q),
                                       gate_bias[:, :, :], ALU.add))
                carry_wait()
                for q in range(Q):
                    last = dve.max(top[:, q, :], logits[:, q, :])
                then(last)
                dve.tensor_tensor(gap[:, :], top[:, :, 1], top[:, :, 0], ALU.subtract).then_inc(gap_ready, 1)
                for q in range(Q):
                    last = dve.max_index(top_at[:, q, :], top[:, q, :], logits[:, q, :])
                then(last)
                then(dve.tensor_copy(top_f[:, :, :], top_at[:, :, 0:2]))
                for j in range(2):
                    last = dve.tensor_tensor(hot[:, j, :, :], iota, wide(top_f[:, :, j:j + 1]), ALU.is_equal)
                dve.wait_ge(egap_ready, b)
                then(dve.tensor_scalar(den[:, :], egap[:, :], 1.0, None, ALU.add))
                then(dve.reciprocal(wt[:, 0, :], den[:, :]))
                then(dve.tensor_tensor(wt[:, 1, :], egap[:, :], wt[:, 0, :], ALU.mult))
                for j in range(2):
                    last = dve.tensor_tensor(hot[:, j, :, :], hot[:, j, :, :],
                                             wide(wt[:, j, :].unsqueeze(2)), ALU.mult)
                then(last)
                then(dve.tensor_tensor(comb[:, :, :], hot[:, 0, :, :], hot[:, 1, :, :], ALU.add))
                then(dve.tensor_copy(comb_hi[:, :, :], comb[:, :, :]))
                dve.tensor_copy(comb_two[:, :, 0:E], comb_hi[:, :, :].bitcast(F32))
                dve.tensor_tensor(comb_two[:, :, E:2 * E], comb[:, :, :], comb_hi[:, :, :].bitcast(F32),
                                  ALU.subtract).then_inc(comb_ready, 1)
                assert step[0] == ROUTER_STEPS

            def weigh(b, k):
                dve.wait_ge(hid_done, b * HC + (k + 1 - HC))
                if k >= 2:
                    dve.wait_ge(hid_lo_made, b * HC + (k - 1 - HC))
                if k % 2 == 0:
                    dve.wait_ge(wgt_copied, b * E + (k // 2 + 1 - E))
                dve.scalar_tensor_tensor(out=pre[:, k % 2, 0:BLOCK], in0=hid[k % HB][:, 0:BLOCK], scalar=b1[:, k:k + 1],
                                         in1=wgt_sb[:, k // 2 % 2, :], op0=ALU.add, op1=ALU.mult)\
                   .then_inc(pre_ready, 1)

            def lo_hidden(b, k):
                dve.wait_ge(hid_hi_made, b * HC + (k + 1 - HC))
                dve.scalar_tensor_tensor(out=hid_lo[:, k % HR, :], in0=pre[:, k % 2, 0:BLOCK], scalar=0.0,
                                         in1=hid_hi[:, k % HR, :], op0=ALU.max, op1=ALU.subtract)\
                   .then_inc(hid_lo_made, 1)

            def iteration(b, adj, prev, next_adj):
                for c in range(CH):
                    if adj and c + 1 < CH:
                        lo(b, c + 1)
                    elif next_adj and c + 1 == CH:
                        lo(b + 1, 0)
                    if prev and c == chunk_of(TURN_X1):
                        dve.wait_ge(x1_turned, b)
                        if not (isinstance(b, int) and b == 1):
                            dve.wait_ge(out_stored, b * 16 - 16)
                        layernorm(lambda q: turn_a[0:QU, q * D:(q + 1) * D], 0, b - 1, x1_stats, x1_rstd, x1_normed)
                    if prev and c == chunk_of(TURN_LN):
                        dve.wait_ge(ln_hi_made, b)
                        dve.tensor_tensor(ln_lo[:, :], turn_b[:, 0:BLOCK], ln_hi[:, :], ALU.subtract)\
                           .then_inc(ln_lo_made, 1)
                    if prev and c == chunk_of(GATE):
                        route(b)
                    if prev:
                        for k in range(HC):
                            if chunk_of(LAYER1[k]) == c:
                                weigh(b, k)
                                if k >= 1:
                                    lo_hidden(b, k - 1)
                        if c == chunk_of(LAYER1[HC - 1]):
                            lo_hidden(b, HC - 1)
                    if adj and c == chunk_of(TURN_X) - 2:
                        dve.wait_ge(x_loaded, b * 16 + 16)
                        layernorm(lambda q: rows3[:, q, :], 1, b, x_stats, x_rstd, x_normed)
                if prev:
                    dve.wait_ge(y_done, b)
                    dve.tensor_tensor(rows[:, 0:BLOCK], y[:, 0:BLOCK], x1T[:, :], ALU.add).then_inc(out_ready, 1)
                if adj:
                    dve.wait_ge(acc_read, b + 1)
                    if prev:
                        dve.wait_ge(out_ready, b)
                    dve.wait_ge(xT_loaded, b * 16 + 16)
                    dve.tensor_tensor(x1T[:, :], cols[:, :], xT_sb[:, :], ALU.add).then_inc(x1_ready, 1)

            dve.wait_ge(const_loaded, 64)
            dve.tensor_tensor(gate_bias[:, :, :], bg, bias, ALU.add).then_inc(small_made, 1)
            dve.wait_ge(small_made, 3)
            dve.tensor_tensor(b2_lo[:, :], b2_raw, b2_hi[:, :], ALU.subtract).then_inc(small_made, 1)
            for g in range(GROUPS + 1):
                if g < GROUPS:
                    n = min(4, TILES - 4 * g) * D
                    dve.wait_ge(h_made, g + 1)
                    if g >= 2:
                        dve.wait_ge(h_lo_made, g - 1)
                    dve.tensor_tensor(pre[:, g % 2, 0:n], hid[g % 2][:, 0:n], rows[:, 0:n], ALU.add)\
                       .then_inc(h_full, 1)
                if g >= 1:
                    n = min(4, TILES - 4 * (g - 1))
                    dve.wait_ge(h_hi_made, g)
                    dve.tensor_tensor(h_lo[:, 4 * (g - 1):4 * (g - 1) + n, :].rearrange("p t d -> p (t d)"),
                                      pre[:, (g - 1) % 2, 0:n * D],
                                      h_hi[:, 4 * (g - 1):4 * (g - 1) + n, :].rearrange("p t d -> p (t d)"),
                                      ALU.subtract).then_inc(h_lo_made, 1)
            for i in range(WEIGHT_LOADS):
                m = ITEM_LOADS + i
                dve.wait_ge(w_hi_made, i + 1)
                at = slice((i % 2) * HALF, (i % 2 + 1) * HALF)
                dve.tensor_tensor((w1_lo if i < 2 else w2_lo)[:, at], raw[:, m % RING, 0:HALF],
                                  (w1_hi if i < 2 else w2_hi)[:, at], ALU.subtract).then_inc(w_lo_made, 1)
            lo(0, 0)
            iteration(0, True, False, True)
            iteration(1, True, True, True)
            with dve.Fori(2, BLOCKS - 1) as b:
                iteration(b, True, True, True)
            iteration(BLOCKS - 1, True, True, False)
            iteration(BLOCKS, False, True, False)


def kernel(**inputs):
    import numpy as np
    import concourse.bacc as bacc
    from concourse.bass_utils import run_bass_kernel_spmd as run

    a = {k: np.asarray(v) for k, v in inputs.items()}
    x, adj = a["x"], a["adj"]
    f32 = np.float32
    pad = TILES * P - N
    adj_t = np.zeros((BLOCKS, P, TILES, BLOCK), f32)
    for b in range(BLOCKS):
        rows_t = np.zeros((TILES * P, BLOCK), f32)
        rows_t[:N] = adj[b * BLOCK:(b + 1) * BLOCK].T
        adj_t[b] = rows_t.reshape(TILES, P, BLOCK).transpose(1, 0, 2)
    item_t = np.pad(a["L0_gnn_item_feat"], ((0, pad), (0, 0))).T
    x_rows = x.reshape(BLOCKS, Q, QU, D).transpose(0, 2, 1, 3).reshape(BLOCKS, QU, Q * D)
    x_t = x.reshape(BLOCKS, BLOCK, D).transpose(0, 2, 1)
    consts = np.zeros((P, C_END), f32)
    consts[:, C_ID:C_ID + P] = np.eye(P, dtype=f32)
    consts[:, C_WU:C_WU + D] = a["L0_gnn_W_user"].T
    consts[:, C_WG:C_WG + E] = a["L0_ffn_Wg"]
    consts[:, C_B1:C_B1 + HC] = a["L0_ffn_b1"].reshape(HC, P).T
    consts[:, C_BU] = a["L0_gnn_b_user"]
    consts[:, C_IOTA:C_IOTA + Q * E] = np.tile(np.arange(E, dtype=f32), Q)
    start = np.zeros((P, S_END), f32)
    start[:, S_WI:S_WI + D] = a["L0_gnn_W_item"].T
    start[0:2 * E, S_B2:S_B2 + D] = np.concatenate([a["L0_ffn_b2"], a["L0_ffn_b2"]], axis=0)
    start[:, S_BG:S_BG + Q * E] = np.tile(a["L0_ffn_bg"], Q)
    start[:, S_BIAS:S_BIAS + Q * E] = np.tile(a["L0_ffn_bias"], Q)
    selectors = np.zeros((2, E, E, P), f32)
    for e in range(E):
        selectors[:, e, e, :] = 1.0
    arrays = {
        "adjT": adj_t.reshape(BLOCKS, P, TILES * BLOCK),
        "itemT": item_t,
        "x": x_rows,
        "xT": x_t,
        "w1": a["L0_ffn_W1"].transpose(1, 0, 2).reshape(D, E * H),
        "w2": a["L0_ffn_W2"].reshape(HC, P, D).transpose(1, 0, 2).reshape(P, HC * D),
        "consts": consts,
        "item_bias": np.tile(a["L0_gnn_b_item"], (P, 4)),
        "selectors": selectors.reshape(2 * E, E * P),
        "start": start,
    }
    nc = bacc.Bacc("TRN2", target_bir_lowering=False, num_devices=1, dynamic_dma_scratch_size=1024)
    feed, args = {}, []
    for name, array in arrays.items():
        feed[name + "_dram"] = np.ascontiguousarray(array)
        args.append(nc.dram_tensor(name + "_dram", array.shape, F32, kind="ExternalInput").ap())
    args.append(nc.dram_tensor("outT_dram", (BLOCKS, D, BLOCK), F32, kind="ExternalOutput").ap())
    build(nc, *args)
    r = run(nc, [feed], core_ids=[0])
    out_t = r.results[0]["outT_dram"].reshape(BLOCKS, D, BLOCK)
    return np.ascontiguousarray(out_t.transpose(0, 2, 1).reshape(N, D))
```

```python
from contextlib import ExitStack

import concourse.bass as bass
from concourse import mybir

F32 = mybir.dt.float32
F32R = mybir.dt.float32r
U32 = mybir.dt.uint32
ALU = mybir.AluOpType
ACT = mybir.ActivationFunctionType

P = 128
N = 10000
D = 128
E = 8
H = 256
HC = E * H // P
BLOCK = 500
BLOCKS = N // BLOCK
Q = 4
QU = BLOCK // Q
TILES = -(-N // P)
CHUNKS = [3] * 23 + [2] * 5
CH = len(CHUNKS)
FIRST = [sum(CHUNKS[:c]) for c in range(CH + 1)]
RAWS = 4
RING = 4
AHEAD_HI, AHEAD_LO = 3, 2
assert sum(CHUNKS) == TILES and CH % RING == 0 and CH % RAWS == 0
ITEM_TILES = 10
ITEM_LOADS = -(-TILES // ITEM_TILES)
GROUPS = -(-TILES // 4)
WEIGHT_LOADS = 4
QUARTER = HC * P // WEIGHT_LOADS
RAW0 = ITEM_LOADS + WEIGHT_LOADS
assert RAW0 % RAWS == 0
HR = 4
EPS = 1e-5

TURN_X1, TURN_LN, GATE, TURN_C, EXPERTS, TURN_X, USER = 4, 12, 16, 26, 27, 60, 74
LAYER1 = [EXPERTS + round(2.9 * k) for k in range(HC)]
LOAD_X = 12
LAG = 2

C_ID, C_WU, C_WG, C_B1, C_BU, C_IOTA, C_END = 0, 128, 256, 264, 280, 281, 313
S_WI, S_B2, S_BG, S_BIAS, S_END = 0, 128, 256, 288, 320


def chunk_of(slot):
    return next(c for c in range(CH) if slot < FIRST[c + 1])


def build(nc, adjT, itemT, x, xT, w1, w2, consts, item_bias, selectors, start, outT):
    with ExitStack() as ctx:
        def sb(name, shape, dt=F32):
            return ctx.enter_context(nc.sbuf_tensor(name, shape, dt))

        def ps(name, shape):
            return ctx.enter_context(nc.psum_tensor(name, shape, F32))

        def sem(name):
            return ctx.enter_context(nc.semaphore(name))

        raw = sb("raw", [P, RAWS, max(CHUNKS) * BLOCK])
        adj_hi = sb("adj_hi", [P, RING, max(CHUNKS) * BLOCK], F32R)
        adj_lo = sb("adj_lo", [P, RING, max(CHUNKS) * BLOCK], F32R)
        h_hi = sb("h_hi", [P, TILES, D], F32R)
        h_lo = sb("h_lo", [P, TILES, D], F32R)
        w1_hi = sb("w1_hi", [P, HC * P], F32R)
        w1_lo = sb("w1_lo", [P, HC * P], F32R)
        w2_sb = sb("w2_sb", [P, HC * P])
        cst = sb("cst", [P, C_END])
        gate_bias = sb("gate_bias", [QU, Q, E])
        select = sb("select", [2 * E, E, P], F32R)
        b2_hi = sb("b2_hi", [2 * E, D], F32R)
        b2_lo = sb("b2_lo", [2 * E, D], F32R)
        rows = sb("rows", [P, Q * D])
        cols = sb("cols", [P, BLOCK])
        xT_sb = sb("xT_sb", [P, BLOCK])
        x1T = sb("x1T", [P, BLOCK])
        ln_hi = sb("ln_hi", [P, BLOCK], F32R)
        ln_lo = sb("ln_lo", [P, BLOCK], F32R)
        pre = sb("pre", [P, 2, Q * D])
        hid_sb = sb("hid_sb", [P, HR, BLOCK])
        stats = sb("stats", [QU, 2, Q, 6])
        moments = sb("moments", [QU, 2, Q, 2])
        var_eps = sb("var_eps", [QU, 2, Q])
        rstd = sb("rstd", [QU, 2, Q])
        spacer = sb("spacer", [1, 1])
        minus_half = sb("minus_half", [QU, Q])
        logits = sb("logits", [QU, Q, E])
        top = sb("top", [QU, Q, 8])
        top_at = sb("top_at", [QU, Q, 8], U32)
        top_f = sb("top_f", [QU, Q, 2])
        gap = sb("gap", [QU, Q])
        egap = sb("egap", [QU, Q])
        den = sb("den", [QU, Q])
        wt = sb("wt", [QU, 2, Q])
        hot = sb("hot", [QU, 2, Q, E])
        comb = sb("comb", [QU, Q, E])
        comb_hi = sb("comb_hi", [QU, Q, E], F32R)
        comb_two = sb("comb_two", [QU, Q, 2 * E])
        combT = sb("combT", [2 * E, BLOCK], F32R)

        ident = cst[:, C_ID:C_ID + P]
        wiT = xT_sb[:, S_WI:S_WI + D]
        b2_raw = xT_sb[0:2 * E, S_B2:S_B2 + D]
        wuT = cst[:, C_WU:C_WU + D]
        wg = cst[:, C_WG:C_WG + E]
        b1 = cst[:, C_B1:C_B1 + HC]
        b_user = cst[:, C_BU:C_BU + 1]
        iota = cst[0:QU, C_IOTA:C_IOTA + Q * E].rearrange("p (q e) -> p q e", q=Q)
        bg = xT_sb[0:QU, S_BG:S_BG + Q * E].rearrange("p (q e) -> p q e", q=Q)
        bias = xT_sb[0:QU, S_BIAS:S_BIAS + Q * E].rearrange("p (q e) -> p q e", q=Q)
        rows3 = rows[0:QU, :].rearrange("p (q d) -> p q d", q=Q)

        acc = ps("acc", [P, 512])
        y = ps("y", [P, 512])
        hid = [ps(f"hid{i}", [P, 512]) for i in range(2)]
        wgt = [ps(f"wgt{i}", [P, 512]) for i in range(2)]
        turn_a = ps("turn_a", [P, 512])
        turn_b = ps("turn_b", [P, 512])

        const_loaded = sem("const_loaded")
        raw_loaded = [sem(f"raw_loaded{i}") for i in range(RAWS)]
        item_used = sem("item_used")
        h_made = sem("h_made")
        h_full = sem("h_full")
        h_hi_made = sem("h_hi_made")
        h_lo_made = sem("h_lo_made")
        w_hi_made = sem("w_hi_made")
        w_lo_made = sem("w_lo_made")
        half_made = sem("half_made")
        w2_loaded = sem("w2_loaded")
        small_made = sem("small_made")
        hi_ready = sem("hi_ready")
        lo_ready = sem("lo_ready")
        chunk_used = sem("chunk_used")
        acc_done = sem("acc_done")
        acc_read = sem("acc_read")
        x_loaded = sem("x_loaded")
        xT_loaded = sem("xT_loaded")
        x_stats = sem("x_stats")
        x_rstd = sem("x_rstd")
        x_normed = sem("x_normed")
        x_turned = sem("x_turned")
        xcols_ready = sem("xcols_ready")
        x1_ready = sem("x1_ready")
        x1_turned = sem("x1_turned")
        x1_stats = sem("x1_stats")
        x1_rstd = sem("x1_rstd")
        x1_normed = sem("x1_normed")
        ln_turned = sem("ln_turned")
        ln_cols = sem("ln_cols")
        ln_hi_made = sem("ln_hi_made")
        ln_lo_made = sem("ln_lo_made")
        gate_done = sem("gate_done")
        router = sem("router")
        gap_ready = sem("gap_ready")
        egap_ready = sem("egap_ready")
        comb_ready = sem("comb_ready")
        comb_turned = sem("comb_turned")
        combT_ready = sem("combT_ready")
        wgt_done = sem("wgt_done")
        hid_done = sem("hid_done")
        pre_ready = sem("pre_ready")
        hid_ready = sem("hid_ready")
        hid_used = sem("hid_used")
        y_done = sem("y_done")
        out_ready = sem("out_ready")
        out_stored = sem("out_stored")
        ROUTER_STEPS = 11
        SMALL = 4

        block = ctx.enter_context(nc.Block())

        @block.sync
        def _(sp):
            sp.dma_start(cst[:, :], consts).then_inc(const_loaded, 16)
            sp.dma_start(rows[:, :], item_bias).then_inc(const_loaded, 16)
            sp.dma_start(pre[0:2 * E, :, :].rearrange("p a b -> p (a b)"), selectors).then_inc(const_loaded, 16)
            sp.dma_start(xT_sb[:, 0:S_END], start).then_inc(const_loaded, 16)

            def load_start(m):
                if m >= RAWS:
                    if m - RAWS < ITEM_LOADS:
                        sp.wait_ge(item_used, m - RAWS + 1)
                    else:
                        sp.wait_ge(w_lo_made, m - RAWS - ITEM_LOADS + 1)
                if m < ITEM_LOADS:
                    t0, t1 = m * ITEM_TILES, min((m + 1) * ITEM_TILES, TILES)
                    src = itemT[:, t0 * P:t1 * P]
                else:
                    i = m - ITEM_LOADS
                    src = w1[:, i * QUARTER:(i + 1) * QUARTER]
                sp.dma_start(raw[:, m % RAWS, 0:src.shape[1]], src).then_inc(raw_loaded[m % RAWS], 16)

            def load_adj(b, c):
                src = adjT[bass.ds(b, 1), :, FIRST[c] * BLOCK:FIRST[c + 1] * BLOCK].rearrange("a p n -> (a p) n")
                sp.dma_start(raw[:, c % RAWS, 0:CHUNKS[c] * BLOCK], src).then_inc(raw_loaded[c % RAWS], 16)

            def iteration(b, adj, next_adj, store):
                for c in range(CH):
                    if c + RAWS < CH and adj:
                        sp.wait_ge(lo_ready, b * CH + (c + 1))
                        load_adj(b, c + RAWS)
                    elif c + RAWS >= CH and next_adj:
                        sp.wait_ge(lo_ready, b * CH + (c + 1))
                        load_adj(b + 1, c + RAWS - CH)
                    if c == 1 and store:
                        sp.wait_ge(out_ready, b - 1)
                        sp.dma_start(outT[bass.ds(b - 2, 1), :, :].rearrange("a p n -> (a p) n"),
                                     rows[:, 0:BLOCK]).then_inc(out_stored, 16)
                    if c == LOAD_X and adj:
                        if isinstance(b, int) and b == 0:
                            sp.wait_ge(h_full, GROUPS)
                        else:
                            sp.wait_ge(ln_turned, b)
                            sp.wait_ge(x1_ready, b)
                        sp.dma_start(rows3, x[bass.ds(b, 1), :, :].rearrange("a p (q d) -> (a p) q d", q=Q))\
                          .then_inc(x_loaded, 16)
                        sp.dma_start(xT_sb[:, :], xT[bass.ds(b, 1), :, :].rearrange("a p n -> (a p) n"))\
                          .then_inc(xT_loaded, 16)

            for m in range(RAW0):
                load_start(m)
            sp.dma_start(w2_sb[:, :], w2).then_inc(w2_loaded, 16)
            for c in range(RAWS):
                sp.wait_ge(w_lo_made, c + 1)
                load_adj(0, c)
            iteration(0, True, True, False)
            iteration(1, True, True, False)
            with sp.Fori(2, BLOCKS - 1) as b:
                iteration(b, True, True, True)
            iteration(BLOCKS - 1, True, False, True)
            iteration(BLOCKS, False, False, True)
            sp.wait_ge(out_ready, BLOCKS)
            sp.dma_start(outT[BLOCKS - 1], rows[:, 0:BLOCK]).then_inc(out_stored, 16)
            sp.wait_ge(out_stored, 16 * BLOCKS)

        @block.tensor
        def _(pe):
            def product(out, hi, lo, m_hi, m_lo, start, stop):
                pe.matmul(out, hi, m_hi, start=start, stop=False)
                pe.matmul(out, hi, m_lo, start=False, stop=False)
                return pe.matmul(out, lo, m_hi, start=False, stop=stop)

            def make_h():
                pe.wait_ge(const_loaded, 64)
                for g in range(GROUPS):
                    if g >= 2:
                        pe.wait_ge(h_full, g - 1)
                    for t in range(4 * g, min(4 * g + 4, TILES)):
                        m, i = divmod(t, ITEM_TILES)
                        if i == 0:
                            pe.wait_ge(raw_loaded[m % RAWS], 16 * (m // RAWS + 1))
                        mm = pe.matmul(hid[g % 2][:, (t % 4) * D:(t % 4 + 1) * D],
                                       raw[:, m % RAWS, i * P:(i + 1) * P], wiT, start=True, stop=True)
                        if i == ITEM_TILES - 1 or t == TILES - 1:
                            mm.then_inc(item_used, 1)
                            if t % 4 == 3 or t == TILES - 1:
                                pe.drain().then_inc(h_made, 1)
                        elif t % 4 == 3:
                            mm.then_inc(h_made, 1)

            def turn(out, source, rows_in, cols_in, done):
                for q in range(Q):
                    mm = pe.transpose(out(q), source(q), ident[0:rows_in, 0:rows_in])
                mm.then_inc(done, 1)

            def adj_tile(b, t):
                c = chunk_of(t)
                i = t - FIRST[c]
                if i == 0:
                    pe.wait_ge(hi_ready, b * CH + (c + 1))
                    pe.wait_ge(lo_ready, b * CH + (c + 1))
                at = slice(i * BLOCK, (i + 1) * BLOCK)
                mm = product(acc[:, 0:BLOCK], h_hi[:, t, :], h_lo[:, t, :],
                             adj_hi[:, c % RING, at], adj_lo[:, c % RING, at],
                             start=(t == 0), stop=(t == TILES - 1))
                if i == CHUNKS[c] - 1:
                    mm.then_inc(chunk_used, 1)

            def layer1(b, k):
                if k == 0:
                    pe.wait_ge(ln_hi_made, b)
                    pe.wait_ge(ln_lo_made, b)
                if k >= 2:
                    pe.wait_ge(pre_ready, b * HC + (k - 1 - HC))
                at = slice(k * P, (k + 1) * P)
                product(hid[k % 2][:, 0:BLOCK], w1_hi[:, at], w1_lo[:, at], ln_hi[:, :], ln_lo[:, :],
                        start=True, stop=True).then_inc(hid_done, 1)

            def spread_weights(b, e):
                if e == 0:
                    pe.wait_ge(combT_ready, b)
                if e >= 2:
                    pe.wait_ge(hid_ready, b * HC + (2 * (e - 1) - HC))
                pe.matmul(wgt[e % 2][:, 0:BLOCK], select[:, e, :], combT[:, :],
                          start=True, stop=True).then_inc(wgt_done, 1)

            def layer2(b, k):
                pe.wait_ge(hid_ready, b * HC + (k + 1 - HC))
                pe.matmul(y[:, 0:BLOCK], w2_sb[:, k * P:(k + 1) * P], hid_sb[:, k % HR, :],
                          start=(k == 0), stop=False).then_inc(hid_used, 1)

            def iteration(b, adj, prev):
                for s in range(TILES):
                    if adj:
                        if s == 0 and prev:
                            pe.wait_ge(acc_read, b)
                        adj_tile(b, s)
                    if prev and s == TURN_X1:
                        pe.wait_ge(x1_ready, b)
                        turn(lambda q: turn_a[0:QU, q * D:(q + 1) * D],
                             lambda q: x1T[:, q * QU:(q + 1) * QU], P, QU, x1_turned)
                    if prev and s == TURN_LN:
                        pe.wait_ge(x1_normed, b)
                        turn(lambda q: turn_b[:, q * QU:(q + 1) * QU], lambda q: rows3[:, q, :], QU, D, ln_turned)
                    if prev and s == GATE:
                        pe.wait_ge(ln_cols, b)
                        for q in range(Q):
                            mm = pe.matmul(turn_a[0:QU, q * E:(q + 1) * E], cols[:, q * QU:(q + 1) * QU], wg,
                                           start=True, stop=True)
                        mm.then_inc(gate_done, 1)
                    if prev and s == TURN_C:
                        pe.wait_ge(comb_ready, b)
                        turn(lambda q: turn_b[0:2 * E, q * QU:(q + 1) * QU],
                             lambda q: comb_two[:, q, :], QU, 2 * E, comb_turned)
                    for k in range(HC):
                        if prev and s == LAYER1[k]:
                            if k % 2 == 0:
                                spread_weights(b, k // 2)
                            layer1(b, k)
                            if k >= LAG:
                                layer2(b, k - LAG)
                    if adj and s == TURN_X:
                        pe.wait_ge(x_normed, b + 1)
                        turn(lambda q: turn_a[:, q * QU:(q + 1) * QU], lambda q: rows3[:, q, :], QU, D, x_turned)
                    if adj and s == USER:
                        pe.wait_ge(xcols_ready, b + 1)
                        pe.matmul(acc[:, 0:BLOCK], wuT, cols[:, :], start=False, stop=False)
                if adj:
                    pe.drain().then_inc(acc_done, 1)
                if prev:
                    for k in range(HC - LAG, HC):
                        layer2(b, k)
                    pe.matmul(y[:, 0:BLOCK], b2_hi[:, :], combT[:, :], start=False, stop=False)
                    pe.matmul(y[:, 0:BLOCK], b2_lo[:, :], combT[:, :], start=False, stop=True).then_inc(y_done, 1)

            make_h()
            pe.wait_ge(h_hi_made, GROUPS)
            pe.wait_ge(h_lo_made, GROUPS)
            pe.wait_ge(w_hi_made, WEIGHT_LOADS)
            pe.wait_ge(w_lo_made, WEIGHT_LOADS)
            pe.wait_ge(small_made, SMALL)
            pe.wait_ge(w2_loaded, 16)
            iteration(0, True, False)
            with pe.Fori(1, BLOCKS) as b:
                iteration(b, True, True)
            iteration(BLOCKS, False, True)

        @block.scalar
        def _(act):
            def copy(out, in_):
                return act.activation(out, in_, ACT.Copy)

            def hi(b, c):
                act.wait_ge(raw_loaded[c % RAWS], b * (16 * CH // RAWS) + 16 * ((RAW0 + c) // RAWS + 1))
                if not (isinstance(b, int) and b == 0 and c < RING):
                    act.wait_ge(chunk_used, b * CH + (c - RING + 1))
                n = CHUNKS[c] * BLOCK
                copy(adj_hi[:, c % RING, 0:n], raw[:, c % RAWS, 0:n]).then_inc(hi_ready, 1)

            def relu_hidden(b, k):
                act.wait_ge(hid_done, b * HC + (k + 1 - HC))
                if k >= 2:
                    act.wait_ge(hid_ready, b * HC + (k - 1 - HC))
                act.activation(pre[:, k % 2, 0:BLOCK], hid[k % 2][:, 0:BLOCK], ACT.Relu,
                               bias=b1[:, k:k + 1]).then_inc(pre_ready, 1)

            def iteration(b, adj, prev, next_adj):
                for c in range(CH):
                    if adj and c + AHEAD_HI < CH:
                        hi(b, c + AHEAD_HI)
                    elif next_adj and c + AHEAD_HI >= CH:
                        hi(b + 1, c + AHEAD_HI - CH)
                    if adj and c == CH - 1:
                        act.wait_ge(acc_done, b + 1)
                        act.activation(cols[:, :], acc[:, 0:BLOCK], ACT.Relu, bias=b_user).then_inc(acc_read, 1)
                    if prev and c == chunk_of(TURN_LN):
                        act.wait_ge(ln_turned, b)
                        copy(ln_hi[:, :], turn_b[:, 0:BLOCK]).then_inc(ln_hi_made, 1)
                        copy(cols[:, :], turn_b[:, 0:BLOCK]).then_inc(ln_cols, 1)
                    if prev and c == chunk_of(GATE) + 2:
                        act.wait_ge(gap_ready, b)
                        act.activation(egap[:, :], gap[:, :], ACT.Exp).then_inc(egap_ready, 1)
                    if prev and c == chunk_of(TURN_C):
                        act.wait_ge(comb_turned, b)
                        copy(combT[:, :], turn_b[0:2 * E, 0:BLOCK]).then_inc(combT_ready, 1)
                    if prev:
                        for k in range(HC):
                            if chunk_of(LAYER1[k]) == c:
                                relu_hidden(b, k)
                    if adj and c == chunk_of(TURN_X):
                        act.wait_ge(x_turned, b + 1)
                        copy(cols[:, :], turn_a[:, 0:BLOCK]).then_inc(xcols_ready, 1)

            act.wait_ge(const_loaded, 64)
            copy(select[:, :, :].rearrange("p e m -> p (e m)"),
                 pre[0:2 * E, :, :].rearrange("p a b -> p (a b)")).then_inc(small_made, 1)
            copy(b2_hi[:, :], b2_raw).then_inc(small_made, 1)
            for g in range(GROUPS):
                n = min(4, TILES - 4 * g)
                act.wait_ge(h_full, g + 1)
                copy(h_hi[:, 4 * g:4 * g + n, :].rearrange("p t d -> p (t d)"),
                     pre[:, g % 2, 0:n * D]).then_inc(h_hi_made, 1)
            for i in range(WEIGHT_LOADS):
                m = ITEM_LOADS + i
                act.wait_ge(raw_loaded[m % RAWS], 16 * (m // RAWS + 1))
                copy(w1_hi[:, i * QUARTER:(i + 1) * QUARTER], raw[:, m % RAWS, 0:QUARTER]).then_inc(w_hi_made, 1)
            for c in range(AHEAD_HI):
                hi(0, c)
            iteration(0, True, False, True)
            with act.Fori(1, BLOCKS - 1) as b:
                iteration(b, True, True, True)
            iteration(BLOCKS - 1, True, True, False)
            iteration(BLOCKS, False, True, False)


        @block.gpsimd
        def _(pool):
            def root(i, steps, n, rooted):
                pool.wait_ge(steps, n * 3 + 3)
                pool.tensor_tensor(rstd[:, i, :], var_eps[:, i, :], minus_half[:, :], ALU.pow).then_inc(rooted, 1)

            pool.memset(minus_half[:, :], -0.5).then_inc(half_made, 1)
            pool.wait_ge(half_made, 1)
            root(1, x_stats, 0, x_rstd)
            with pool.Fori(1, BLOCKS) as b:
                root(0, x1_stats, b - 1, x1_rstd)
                root(1, x_stats, b, x_rstd)
            root(0, x1_stats, BLOCKS - 1, x1_rstd)

        @block.vector
        def _(dve):
            def lo(b, c):
                dve.wait_ge(hi_ready, b * CH + (c + 1))
                n = CHUNKS[c] * BLOCK
                dve.tensor_tensor(adj_lo[:, c % RING, 0:n], raw[:, c % RAWS, 0:n],
                                  adj_hi[:, c % RING, 0:n], ALU.subtract).then_inc(lo_ready, 1)

            def carry_wait():
                dve.memset(spacer[:, :], 0.0)

            def layernorm(source, i, n, steps, rooted, done):
                for q in range(Q):
                    last = dve.bn_stats(stats[:, i, q, :], source(q))
                last.then_inc(steps, 1)
                dve.wait_ge(steps, n * 3 + 1)
                carry_wait()
                for q in range(Q):
                    last = dve.bn_aggr(moments[:, i, q, :], stats[:, i, q, :])
                last.then_inc(steps, 1)
                dve.wait_ge(steps, n * 3 + 2)
                dve.tensor_scalar(var_eps[:, i, :], moments[:, i, :, 1], EPS, None, ALU.add).then_inc(steps, 1)
                dve.wait_ge(rooted, n + 1)
                for q in range(Q):
                    last = dve.tensor_scalar(rows3[:, q, :], source(q), moments[:, i, q, 0:1],
                                             rstd[:, i, q:q + 1], ALU.subtract, ALU.mult)
                last.then_inc(done, 1)

            def wide(v):
                return v.broadcast_to([QU, Q, E])

            def router_steps(b, step):
                def then(instruction):
                    nonlocal step
                    step += 1
                    instruction.then_inc(router, 1)
                    dve.wait_ge(router, b * ROUTER_STEPS + (step - ROUTER_STEPS))
                return then

            def route_top(b):
                then = router_steps(b, 0)
                dve.wait_ge(gate_done, b)
                then(dve.tensor_tensor(logits[:, :, :], turn_a[0:QU, 0:Q * E].rearrange("p (q e) -> p q e", q=Q),
                                       gate_bias[:, :, :], ALU.add))
                carry_wait()
                for q in range(Q):
                    last = dve.max(top[:, q, :], logits[:, q, :])
                then(last)
                dve.tensor_tensor(gap[:, :], top[:, :, 1], top[:, :, 0], ALU.subtract).then_inc(gap_ready, 1)
                for q in range(Q):
                    last = dve.max_index(top_at[:, q, :], top[:, q, :], logits[:, q, :])
                then(last)
                then(dve.tensor_copy(top_f[:, :, :], top_at[:, :, 0:2]))
                for j in range(2):
                    last = dve.tensor_tensor(hot[:, j, :, :], iota, wide(top_f[:, :, j:j + 1]), ALU.is_equal)
                last.then_inc(router, 1)

            def route_weights(b):
                then = router_steps(b, 5)
                dve.wait_ge(egap_ready, b)
                then(dve.tensor_scalar(den[:, :], egap[:, :], 1.0, None, ALU.add))
                then(dve.reciprocal(wt[:, 0, :], den[:, :]))
                then(dve.tensor_tensor(wt[:, 1, :], egap[:, :], wt[:, 0, :], ALU.mult))
                for j in range(2):
                    last = dve.tensor_tensor(hot[:, j, :, :], hot[:, j, :, :],
                                             wide(wt[:, j, :].unsqueeze(2)), ALU.mult)
                then(last)
                then(dve.tensor_tensor(comb[:, :, :], hot[:, 0, :, :], hot[:, 1, :, :], ALU.add))
                then(dve.tensor_copy(comb_hi[:, :, :], comb[:, :, :]))
                dve.tensor_copy(comb_two[:, :, 0:E], comb_hi[:, :, :].bitcast(F32))
                dve.tensor_tensor(comb_two[:, :, E:2 * E], comb[:, :, :], comb_hi[:, :, :].bitcast(F32),
                                  ALU.subtract).then_inc(comb_ready, 1)

            def weigh(b, k):
                dve.wait_ge(pre_ready, b * HC + (k + 1 - HC))
                if k % 2 == 0:
                    dve.wait_ge(wgt_done, b * E + (k // 2 + 1 - E))
                if k >= HR:
                    dve.wait_ge(hid_used, b * HC + (k - HR + 1 - HC))
                dve.tensor_tensor(hid_sb[:, k % HR, :], pre[:, k % 2, 0:BLOCK], wgt[k // 2 % 2][:, 0:BLOCK],
                                  ALU.mult).then_inc(hid_ready, 1)

            def iteration(b, adj, prev, next_adj):
                for c in range(CH):
                    if adj and c + AHEAD_LO < CH:
                        lo(b, c + AHEAD_LO)
                    elif next_adj and c + AHEAD_LO >= CH:
                        lo(b + 1, c + AHEAD_LO - CH)
                    if prev and c == chunk_of(TURN_X1):
                        dve.wait_ge(x1_turned, b)
                        if not (isinstance(b, int) and b == 1):
                            dve.wait_ge(out_stored, b * 16 - 16)
                        layernorm(lambda q: turn_a[0:QU, q * D:(q + 1) * D], 0, b - 1, x1_stats, x1_rstd, x1_normed)
                    if prev and c == chunk_of(TURN_LN):
                        dve.wait_ge(ln_cols, b)
                        dve.tensor_tensor(ln_lo[:, :], cols[:, :], ln_hi[:, :], ALU.subtract)\
                           .then_inc(ln_lo_made, 1)
                    if prev and c == chunk_of(GATE) + 1:
                        route_top(b)
                    if prev and c == chunk_of(GATE) + 2:
                        route_weights(b)
                    if prev:
                        for k in range(HC):
                            if chunk_of(LAYER1[k]) == c:
                                weigh(b, k)
                    if adj and c == chunk_of(TURN_X) - 3:
                        dve.wait_ge(x_loaded, b * 16 + 16)
                        layernorm(lambda q: rows3[:, q, :], 1, b, x_stats, x_rstd, x_normed)
                if prev:
                    dve.wait_ge(y_done, b)
                    dve.tensor_tensor(rows[:, 0:BLOCK], y[:, 0:BLOCK], x1T[:, :], ALU.add).then_inc(out_ready, 1)
                if adj:
                    dve.wait_ge(acc_read, b + 1)
                    if prev:
                        dve.wait_ge(out_ready, b)
                    dve.wait_ge(xT_loaded, b * 16 + 16)
                    dve.tensor_tensor(x1T[:, :], cols[:, :], xT_sb[:, :], ALU.add).then_inc(x1_ready, 1)

            dve.wait_ge(const_loaded, 64)
            dve.tensor_tensor(gate_bias[:, :, :], bg, bias, ALU.add).then_inc(small_made, 1)
            dve.wait_ge(small_made, 3)
            dve.tensor_tensor(b2_lo[:, :], b2_raw, b2_hi[:, :], ALU.subtract).then_inc(small_made, 1)
            for g in range(GROUPS + 1):
                if g < GROUPS:
                    n = min(4, TILES - 4 * g) * D
                    dve.wait_ge(h_made, g + 1)
                    if g >= 2:
                        dve.wait_ge(h_lo_made, g - 1)
                    dve.tensor_tensor(pre[:, g % 2, 0:n], hid[g % 2][:, 0:n], rows[:, 0:n], ALU.add)\
                       .then_inc(h_full, 1)
                if g >= 1:
                    n = min(4, TILES - 4 * (g - 1))
                    dve.wait_ge(h_hi_made, g)
                    dve.tensor_tensor(h_lo[:, 4 * (g - 1):4 * (g - 1) + n, :].rearrange("p t d -> p (t d)"),
                                      pre[:, (g - 1) % 2, 0:n * D],
                                      h_hi[:, 4 * (g - 1):4 * (g - 1) + n, :].rearrange("p t d -> p (t d)"),
                                      ALU.subtract).then_inc(h_lo_made, 1)
            for i in range(WEIGHT_LOADS):
                m = ITEM_LOADS + i
                dve.wait_ge(w_hi_made, i + 1)
                at = slice(i * QUARTER, (i + 1) * QUARTER)
                dve.tensor_tensor(w1_lo[:, at], raw[:, m % RAWS, 0:QUARTER], w1_hi[:, at],
                                  ALU.subtract).then_inc(w_lo_made, 1)
            for c in range(AHEAD_LO):
                lo(0, c)
            iteration(0, True, False, True)
            iteration(1, True, True, True)
            with dve.Fori(2, BLOCKS - 1) as b:
                iteration(b, True, True, True)
            iteration(BLOCKS - 1, True, True, False)
            iteration(BLOCKS, False, True, False)


def kernel(**inputs):
    import numpy as np
    import concourse.bacc as bacc
    from concourse.bass_utils import run_bass_kernel_spmd as run

    a = {k: np.asarray(v) for k, v in inputs.items()}
    x, adj = a["x"], a["adj"]
    f32 = np.float32
    pad = TILES * P - N
    adj_t = np.zeros((BLOCKS, P, TILES, BLOCK), f32)
    for b in range(BLOCKS):
        rows_t = np.zeros((TILES * P, BLOCK), f32)
        rows_t[:N] = adj[b * BLOCK:(b + 1) * BLOCK].T
        adj_t[b] = rows_t.reshape(TILES, P, BLOCK).transpose(1, 0, 2)
    item_t = np.pad(a["L0_gnn_item_feat"], ((0, pad), (0, 0))).T
    x_rows = x.reshape(BLOCKS, Q, QU, D).transpose(0, 2, 1, 3).reshape(BLOCKS, QU, Q * D)
    x_t = x.reshape(BLOCKS, BLOCK, D).transpose(0, 2, 1)
    consts = np.zeros((P, C_END), f32)
    consts[:, C_ID:C_ID + P] = np.eye(P, dtype=f32)
    consts[:, C_WU:C_WU + D] = a["L0_gnn_W_user"].T
    consts[:, C_WG:C_WG + E] = a["L0_ffn_Wg"]
    consts[:, C_B1:C_B1 + HC] = a["L0_ffn_b1"].reshape(HC, P).T
    consts[:, C_BU] = a["L0_gnn_b_user"]
    consts[:, C_IOTA:C_IOTA + Q * E] = np.tile(np.arange(E, dtype=f32), Q)
    start = np.zeros((P, S_END), f32)
    start[:, S_WI:S_WI + D] = a["L0_gnn_W_item"].T
    start[0:2 * E, S_B2:S_B2 + D] = np.concatenate([a["L0_ffn_b2"], a["L0_ffn_b2"]], axis=0)
    start[:, S_BG:S_BG + Q * E] = np.tile(a["L0_ffn_bg"], Q)
    start[:, S_BIAS:S_BIAS + Q * E] = np.tile(a["L0_ffn_bias"], Q)
    selectors = np.zeros((2, E, E, P), f32)
    for e in range(E):
        selectors[:, e, e, :] = 1.0
    arrays = {
        "adjT": adj_t.reshape(BLOCKS, P, TILES * BLOCK),
        "itemT": item_t,
        "x": x_rows,
        "xT": x_t,
        "w1": a["L0_ffn_W1"].transpose(1, 0, 2).reshape(D, E * H),
        "w2": a["L0_ffn_W2"].reshape(HC, P, D).transpose(1, 0, 2).reshape(P, HC * D),
        "consts": consts,
        "item_bias": np.tile(a["L0_gnn_b_item"], (P, 4)),
        "selectors": selectors.reshape(2 * E, E * P),
        "start": start,
    }
    nc = bacc.Bacc("TRN2", target_bir_lowering=False, num_devices=1, dynamic_dma_scratch_size=1024)
    feed, args = {}, []
    for name, array in arrays.items():
        feed[name + "_dram"] = np.ascontiguousarray(array)
        args.append(nc.dram_tensor(name + "_dram", array.shape, F32, kind="ExternalInput").ap())
    args.append(nc.dram_tensor("outT_dram", (BLOCKS, D, BLOCK), F32, kind="ExternalOutput").ap())
    build(nc, *args)
    r = run(nc, [feed], core_ids=[0])
    out_t = r.results[0]["outT_dram"].reshape(BLOCKS, D, BLOCK)
    return np.ascontiguousarray(out_t.transpose(0, 2, 1).reshape(N, D))
```

```python
from contextlib import ExitStack

import concourse.bass as bass
from concourse import mybir

F32 = mybir.dt.float32
F32R = mybir.dt.float32r
U32 = mybir.dt.uint32
ALU = mybir.AluOpType
ACT = mybir.ActivationFunctionType

P = 128
N = 10000
D = 128
E = 8
H = 256
HC = E * H // P
PER = P // E
BLOCK = 512
FULL = N // BLOCK
LAST = N - FULL * BLOCK
BLOCKS = FULL + 1
Q = 4
assert LAST > 0 and BLOCK == Q * P and LAST % (2 * Q) == 0
TILES = -(-N // P)
CHUNKS = [2] * 39 + [1]
CH = len(CHUNKS)
FIRST = [sum(CHUNKS[:c]) for c in range(CH + 1)]
RING, LO_RING = 5, 4
AHEAD_HI, AHEAD_LO = 4, 3
assert sum(CHUNKS) == TILES and CH % RING == 0 and CH % LO_RING == 0
GROUPS = -(-TILES // 4)
HR = 4
SR = 4
ITEMS = HR - 1
H_AHEAD = 3
H_MADE = [4 * (g - H_AHEAD) + 2 for g in range(GROUPS)]
QUARTER = HC * P // 4
EPS = 1e-5
TAIL = N - (TILES - 1) * P
QUAD = 32
assert 0 < TAIL <= QUAD and P == 4 * QUAD
CR = 4 * E

TURN_X1, TURN_LN, GATE, TURN_C, TURN_X, USER = 4, 13, 19, 30, 60, 70
LAYER1 = [31 + 4 * k for k in range(HC)]
LATE = [50 + round(3.67 * k) for k in range(HC)]
TO_SPLIT, TO_LAYER2 = 6, 16
W_LOAD = (0, 2, 4, 6, 8, 10, 16, 18)
W_SPLIT = (5, 7, 9, 11, 13, 15, 21, 22)
LOAD_X, LOAD_XT = 13, 33
assert LAYER1[-1] - TILES < TURN_LN and LATE[-1] - TILES < TURN_C < LAYER1[0]
assert max(LAYER1[-1], LATE[-1]) < TILES + LAYER1[0]

C_ID, C_WU, C_WG, C_B1, C_BU, C_IOTA, C_END = 0, 128, 256, 264, 280, 281, 313
S_WI, S_B2, S_B2_LOW, S_SIGN, S_BG, S_BIAS, S_END = 0, 128, 256, 384, 385, 417, 449


def chunk_of(slot):
    return next(c for c in range(CH) if slot < FIRST[c + 1])


def width(b):
    return LAST if isinstance(b, int) and b == BLOCKS - 1 else BLOCK


def layer1_slots(b, age):
    late = isinstance(b, int) and b - age == FULL - 1
    return [s - (age - 1) * TILES for s in (LATE if late else LAYER1)]


def result_chunk(b):
    return chunk_of(layer1_slots(b, 2)[-1] + TO_LAYER2)


def build(nc, adjT, adjT_last, itemT, x, x_last, xT, xT_last, w1, w2, consts, item_bias, selector, start,
          outT, outT_last):
    with ExitStack() as ctx:
        def sb(name, shape, dt=F32):
            return ctx.enter_context(nc.sbuf_tensor(name, shape, dt))

        def ps(name):
            return ctx.enter_context(nc.psum_tensor(name, [P, BLOCK], F32))

        def sem(name):
            return ctx.enter_context(nc.semaphore(name))

        raw = sb("raw", [P, RING, max(CHUNKS) * BLOCK])
        adj_hi = sb("adj_hi", [P, RING, max(CHUNKS) * BLOCK], F32R)
        adj_lo = sb("adj_lo", [P, LO_RING, max(CHUNKS) * BLOCK], F32R)
        h_hi = sb("h_hi", [P, TILES, D], F32R)
        h_lo = sb("h_lo", [P, TILES, D], F32R)
        w1_hi = sb("w1_hi", [P, HC * P], F32R)
        w1_lo = sb("w1_lo", [P, HC * P], F32R)
        w2_hi = sb("w2_hi", [P, HC * P], F32R)
        w2_lo = sb("w2_lo", [P, HC * P], F32R)
        cst = sb("cst", [P, C_END])
        gate_bias = sb("gate_bias", [P, Q, E])
        select = sb("select", [CR, P], F32R)
        b2_both = sb("b2_both", [CR, D], F32R)
        rows = sb("rows", [P, Q, D])
        cols = sb("cols", [P, BLOCK])
        xT_sb = sb("xT_sb", [P, BLOCK])
        x1T = sb("x1T", [P, BLOCK])
        x1T_old = sb("x1T_old", [P, BLOCK])
        out_sb = sb("out_sb", [P, BLOCK])
        wu_hi = sb("wu_hi", [P, D], F32R)
        wu_lo = sb("wu_lo", [P, D], F32R)
        xln_hi = sb("xln_hi", [P, BLOCK], F32R)
        xln_lo = sb("xln_lo", [P, BLOCK], F32R)
        ln_hi = sb("ln_hi", [P, BLOCK], F32R)
        ln_lo = sb("ln_lo", [P, BLOCK], F32R)
        pre = sb("pre", [P, 2, BLOCK])
        hid_sb = sb("hid_sb", [P, HR, BLOCK])
        hid_hi = sb("hid_hi", [P, SR, BLOCK], F32R)
        hid_lo = sb("hid_lo", [P, SR, BLOCK], F32R)
        stats = sb("stats", [P, 2, Q, 6])
        moments = sb("moments", [P, 2, Q, 2])
        var_eps = sb("var_eps", [P, 2, Q])
        rstd = sb("rstd", [P, 2, Q])
        shift = sb("shift", [P, 2, Q])
        spacer = sb("spacer", [1, 1])
        minus_half = sb("minus_half", [P, Q])
        logits = sb("logits", [P, Q, E])
        top = sb("top", [P, Q, 8])
        top_at = sb("top_at", [P, Q, 8], U32)
        top_f = sb("top_f", [P, Q, 2])
        gap = sb("gap", [P, Q])
        egap = sb("egap", [P, Q])
        den = sb("den", [P, Q])
        wt = sb("wt", [P, 2, Q])
        hot = sb("hot", [P, 2, Q, E])
        comb = sb("comb", [P, Q, E])
        comb_hi = sb("comb_hi", [P, Q, E], F32R)
        comb_two = sb("comb_two", [P, Q, 2, 2 * E])
        combT = sb("combT", [CR, BLOCK], F32R)

        ident = cst[:, C_ID:C_ID + P]
        wuT = cst[:, C_WU:C_WU + D]
        wg = cst[:, C_WG:C_WG + E]
        b1 = cst[:, C_B1:C_B1 + HC]
        b_user = cst[:, C_BU:C_BU + 1]
        iota = cst[:, C_IOTA:C_IOTA + Q * E].rearrange("p (q e) -> p q e", q=Q)
        wiT = x1T[:, S_WI:S_WI + D]
        b2_raw = x1T[0:CR, S_B2:S_B2 + D]
        b2_low = x1T[0:CR, S_B2_LOW:S_B2_LOW + D]
        b2_sign = x1T[0:CR, S_SIGN:S_SIGN + 1]
        bg = x1T[:, S_BG:S_BG + Q * E].rearrange("p (q e) -> p q e", q=Q)
        bias = x1T[:, S_BIAS:S_BIAS + Q * E].rearrange("p (q e) -> p q e", q=Q)
        item_bc = hid_sb[:, ITEMS, :]
        w_raw = [hid_sb[:, i, :] for i in range(4)] + [out_sb[:, :], xT_sb[:, :]] * 2
        select_raw = x1T_old[0:CR, 0:P]

        acc = ps("acc")
        y = ps("y")
        hid = [ps(f"hid{i}") for i in range(2)]
        wgt = ps("wgt")
        turn_a = ps("turn_a")
        turn_b = ps("turn_b")

        start_loaded = sem("start_loaded")
        bias_loaded = sem("bias_loaded")
        const_loaded = sem("const_loaded")
        select_loaded = sem("select_loaded")
        item_loaded = [sem(f"item_loaded{i}") for i in range(ITEMS)]
        w_loaded = [sem(f"w_loaded{i}") for i in range(8)]
        select_made = sem("select_made")
        small_made = sem("small_made")
        half_made = sem("half_made")
        h_made = sem("h_made")
        h_full = sem("h_full")
        h_hi_made = sem("h_hi_made")
        h_lo_made = sem("h_lo_made")
        h_last_made = sem("h_last_made")
        w_hi_made = sem("w_hi_made")
        w_lo_made = sem("w_lo_made")
        raw_loaded = [sem(f"raw_loaded{i}") for i in range(RING)]
        hi_ready = sem("hi_ready")
        lo_ready = sem("lo_ready")
        chunk_used = sem("chunk_used")
        acc_read = sem("acc_read")
        x_loaded = sem("x_loaded")
        xT_loaded = sem("xT_loaded")
        x_stats = sem("x_stats")
        x_rstd = sem("x_rstd")
        x_shift = sem("x_shift")
        x_normed = sem("x_normed")
        x_turned = sem("x_turned")
        xln_hi_made = sem("xln_hi_made")
        xln_lo_made = sem("xln_lo_made")
        x1_ready = sem("x1_ready")
        x1_turned = sem("x1_turned")
        x1_stats = sem("x1_stats")
        x1_rstd = sem("x1_rstd")
        x1_shift = sem("x1_shift")
        x1_normed = sem("x1_normed")
        ln_turned = sem("ln_turned")
        ln_hi_made = sem("ln_hi_made")
        ln_cols = sem("ln_cols")
        ln_lo_made = sem("ln_lo_made")
        gate_done = sem("gate_done")
        router = sem("router")
        gap_ready = sem("gap_ready")
        egap_ready = sem("egap_ready")
        comb_ready = sem("comb_ready")
        comb_turned = sem("comb_turned")
        combT_ready = sem("combT_ready")
        wgt_done = sem("wgt_done")
        hid_done = sem("hid_done")
        pre_ready = sem("pre_ready")
        hid_ready = sem("hid_ready")
        hid_hi_made = sem("hid_hi_made")
        hid_lo_made = sem("hid_lo_made")
        hid_used = sem("hid_used")
        out_ready = sem("out_ready")
        old_ready = sem("old_ready")
        out_stored = sem("out_stored")
        ROUTER_STEPS = 11
        SMALL = 5

        def upto(b, age, per, i):
            return b * per + (i + 1 - age * per)

        def ln_parts(b, age):
            if isinstance(b, int) and b - age == BLOCKS - 1:
                return adj_hi[:, 0, 0:BLOCK], adj_lo[:, 0, 0:BLOCK]
            return ln_hi[:, :], ln_lo[:, :]

        def sum_bank(b, age):
            return acc if isinstance(b, int) and b - age == BLOCKS - 1 else y

        def before(b, age, k, ring):
            if k >= ring:
                return upto(b, age, HC, k - ring)
            if isinstance(b, int) and b == age:
                return None
            return upto(b, age, HC, max(j for j in range(HC) if j % ring == k) - HC)

        def quarter(i):
            return slice(i % 4 * QUARTER, (i % 4 + 1) * QUARTER)

        block = ctx.enter_context(nc.Block())

        @block.sync
        def _(sp):
            def of(full, last, b):
                if isinstance(b, int) and b == BLOCKS - 1:
                    return last
                return full[bass.ds(b, 1)].rearrange("a p n -> (a p) n")

            def load_items(g):
                if g >= ITEMS:
                    sp.wait_ge(h_made, g - ITEMS + 1)
                n = min(4, TILES - 4 * g) * P
                sp.dma_start(hid_sb[:, g % ITEMS, 0:n], itemT[:, 4 * g * P:4 * g * P + n])\
                  .then_inc(item_loaded[g % ITEMS], 16)

            def load_adj(b, c):
                w = width(b)
                sp.dma_start(raw[:, c % RING, 0:CHUNKS[c] * w],
                             of(adjT, adjT_last, b)[:, FIRST[c] * w:FIRST[c + 1] * w])\
                  .then_inc(raw_loaded[c % RING], 16)

            def load_x(b):
                w = width(b)
                if not (isinstance(b, int) and b == 0):
                    sp.wait_ge(ln_turned, b)
                sp.dma_start(rows[0:w // Q, :, :].rearrange("p q d -> p (q d)"), of(x, x_last, b))\
                  .then_inc(x_loaded, 16)

            def load_xT(b):
                w = width(b)
                if not (isinstance(b, int) and b == 0):
                    sp.wait_ge(x1_ready, b)
                if isinstance(b, int) and b == 1:
                    sp.wait_ge(w_lo_made, 8)
                sp.dma_start(xT_sb[:, 0:w], of(xT, xT_last, b)).then_inc(xT_loaded, 16)

            def store(b, age):
                w = width(b - age)
                sp.wait_ge(out_ready, b - (age - 1))
                sp.dma_start(of(outT, outT_last, b - age), out_sb[:, 0:w]).then_inc(out_stored, 16)

            def iteration(b, adj, next_adj, old):
                for c in range(CH):
                    if c + RING < CH and adj:
                        sp.wait_ge(lo_ready, upto(b, 0, CH, c))
                        load_adj(b, c + RING)
                    elif c + RING >= CH and next_adj:
                        sp.wait_ge(lo_ready, upto(b, 0, CH, c))
                        load_adj(b + 1, c + RING - CH)
                    if adj and c == LOAD_X:
                        load_x(b)
                    if adj and c == LOAD_XT:
                        load_xT(b)
                    if old and c == result_chunk(b) + 3:
                        store(b, 2)
                    if isinstance(b, int) and b == 0:
                        for g in range(ITEMS + H_AHEAD, GROUPS):
                            if c == chunk_of(H_MADE[g - ITEMS]):
                                load_items(g)
                    if isinstance(b, int) and b == 1 and c in W_LOAD:
                        i = W_LOAD.index(c)
                        if i == 0:
                            sp.wait_ge(h_full, GROUPS)
                        if i == 5:
                            sp.wait_ge(x1_ready, 1)
                        if i >= 6:
                            sp.wait_ge(w_lo_made, i - 1)
                        sp.dma_start(w_raw[i], (w1, w2)[i // 4][:, quarter(i)]).then_inc(w_loaded[i], 16)

            sp.dma_start(x1T[:, 0:S_END], start).then_inc(start_loaded, 16)
            load_items(0)
            sp.dma_start(item_bc, item_bias).then_inc(bias_loaded, 16)
            load_adj(0, 0)
            load_items(1)
            load_items(2)
            sp.dma_start(cst[:, :], consts).then_inc(const_loaded, 16)
            sp.dma_start(select_raw, selector).then_inc(select_loaded, 16)
            for c in range(1, RING):
                load_adj(0, c)
                if c <= H_AHEAD:
                    load_items(ITEMS - 1 + c)
            iteration(0, True, True, False)
            iteration(1, True, True, False)
            with sp.Fori(2, BLOCKS - 2) as b:
                iteration(b, True, True, True)
            iteration(BLOCKS - 2, True, True, True)
            iteration(BLOCKS - 1, True, False, True)
            store(BLOCKS, 2)
            store(BLOCKS + 1, 2)
            sp.wait_ge(out_stored, 16 * BLOCKS)

        @block.tensor
        def _(pe):
            def product(out, hi, lo, m_hi, m_lo, start, stop):
                pe.matmul(out, hi, m_hi, start=start, stop=False)
                pe.matmul(out, hi, m_lo, start=False, stop=False)
                return pe.matmul(out, lo, m_hi, start=False, stop=stop)

            def make_h(g):
                if g == 0:
                    pe.wait_ge(start_loaded, 16)
                if g >= 2:
                    pe.wait_ge(h_full, g - 1)
                pe.wait_ge(item_loaded[g % ITEMS], 16 * (g // ITEMS + 1))
                for t in range(min(4, TILES - 4 * g)):
                    mm = pe.matmul(hid[g % 2][:, t * D:(t + 1) * D], hid_sb[:, g % ITEMS, t * P:(t + 1) * P], wiT,
                                   start=True, stop=True)
                mm.then_inc(h_made, 1)

            def turn(out, source, rows_in, done):
                for q in range(Q):
                    mm = pe.transpose(out(q), source(q), ident[0:rows_in, 0:rows_in])
                mm.then_inc(done, 1)

            def adj_tile(b, t):
                w = width(b)
                c = chunk_of(t)
                i = t - FIRST[c]
                if isinstance(b, int) and b == 0 and t % 4 == 0:
                    pe.wait_ge(h_hi_made, t // 4 + 1)
                    pe.wait_ge(h_lo_made, t // 4 + 1)
                if isinstance(b, int) and b == 0 and t == TILES - 1:
                    pe.wait_ge(h_last_made, 1)
                if i == 0:
                    pe.wait_ge(hi_ready, upto(b, 0, CH, c))
                    pe.wait_ge(lo_ready, upto(b, 0, CH, c))
                at = slice(i * w, (i + 1) * w)
                if t < TILES - 1:
                    mm = product(acc[:, 0:w], h_hi[:, t, :], h_lo[:, t, :],
                                 adj_hi[:, c % RING, at], adj_lo[:, c % LO_RING, at], start=(t == 0), stop=False)
                else:
                    mm = pe.matmul(acc[:, 0:w], h_hi[:, t, :], adj_hi[:, c % RING, at], start=False, stop=True)
                if i == CHUNKS[c] - 1:
                    mm.then_inc(chunk_used, 1)

            def gate(b, age):
                u = width(b - age) // Q
                pe.wait_ge(ln_cols, upto(b, age, 1, 0))
                for q in range(Q):
                    mm = pe.matmul(turn_a[0:u, q * E:(q + 1) * E], cols[:, q * u:(q + 1) * u], wg,
                                   start=True, stop=True)
                mm.then_inc(gate_done, 1)

            def layer1(b, age, k):
                w = width(b - age)
                if k == 0:
                    pe.wait_ge(w_lo_made, 4)
                    pe.wait_ge(ln_lo_made, upto(b, age, 1, 0))
                if before(b, age, k, 2) is not None:
                    pe.wait_ge(pre_ready, before(b, age, k, 2))
                at = slice(k * P, (k + 1) * P)
                ln = ln_parts(b, age)
                product(hid[k % 2][:, 0:w], w1_hi[:, at], w1_lo[:, at], ln[0][:, 0:w], ln[1][:, 0:w],
                        start=True, stop=True).then_inc(hid_done, 1)

            def spread_weights(b, age):
                w = width(b - age)
                pe.wait_ge(combT_ready, upto(b, age, 1, 0))
                if not (isinstance(b, int) and b == age):
                    pe.wait_ge(hid_ready, upto(b, age, HC, -1))
                pe.matmul(wgt[:, 0:w], select[:, :], combT[:, 0:w], start=True, stop=True).then_inc(wgt_done, 1)

            def layer2(b, age, k):
                w = width(b - age)
                total = sum_bank(b, age)[:, 0:w]
                if k == 0:
                    if not (isinstance(b, int) and b in (1, BLOCKS)):
                        pe.wait_ge(out_ready, upto(b, 2, 1, 0))
                    pe.matmul(total, b2_both[:, :], combT[:, 0:w], start=True, stop=False)
                pe.wait_ge(hid_lo_made, upto(b, age, HC, k))
                at = slice(k * P, (k + 1) * P)
                if isinstance(b, int) and b == age:
                    pe.wait_ge(w_lo_made, 5 + k // (HC // 4))
                product(total, w2_hi[:, at], w2_lo[:, at], hid_hi[:, k % SR, 0:w], hid_lo[:, k % SR, 0:w],
                        start=False, stop=(k == HC - 1)).then_inc(hid_used, 1)

            def iteration(b, adj, prev, old):
                w = width(b)
                u = width(b - 1) // Q
                for s in range(TILES):
                    if isinstance(b, int) and b == 0 and s in H_MADE:
                        make_h(H_MADE.index(s))
                    if prev and s == TURN_X1:
                        pe.wait_ge(x1_ready, upto(b, 1, 1, 0))
                        turn(lambda q: turn_a[0:u, q * D:(q + 1) * D],
                             lambda q: x1T[:, q * u:(q + 1) * u], P, x1_turned)
                    if prev and s == TURN_LN:
                        pe.wait_ge(x1_normed, upto(b, 1, 1, 0))
                        turn(lambda q: turn_b[:, q * u:(q + 1) * u], lambda q: rows[0:u, q, :], u, ln_turned)
                    if prev and s == GATE:
                        gate(b, 1)
                    if prev and s == TURN_C:
                        pe.wait_ge(comb_ready, upto(b, 1, 1, 0))
                        turn(lambda q: turn_b[0:CR, q * u:(q + 1) * u],
                             lambda q: comb_two[0:u, q, :, :].rearrange("p r e -> p (r e)"), u, comb_turned)
                    for age in (1, 2):
                        for k, slot in enumerate(layer1_slots(b, age)):
                            if (prev, old)[age - 1] and slot == s:
                                layer1(b, age, k)
                            if prev and age == 1 and k == 0 and slot + 1 == s:
                                spread_weights(b, age)
                            if (prev, old)[age - 1] and slot + TO_LAYER2 == s:
                                layer2(b, age, k)
                    if adj and s == TURN_X:
                        pe.wait_ge(x_normed, upto(b, 0, 1, 0))
                        turn(lambda q: turn_a[:, q * (w // Q):(q + 1) * (w // Q)],
                             lambda q: rows[0:w // Q, q, :], w // Q, x_turned)
                    if adj and s == USER:
                        pe.wait_ge(xln_lo_made, upto(b, 0, 1, 0))
                        if isinstance(b, int) and b == 0:
                            pe.wait_ge(small_made, SMALL)
                        product(acc[:, 0:w], wu_hi[:, :], wu_lo[:, :], xln_hi[:, 0:w], xln_lo[:, 0:w],
                                start=False, stop=False)
                    if adj:
                        if s == 0 and prev:
                            pe.wait_ge(acc_read, upto(b, 1, 1, 0))
                        adj_tile(b, s)

            for g in range(H_AHEAD):
                make_h(g)
            pe.wait_ge(const_loaded, 16)
            iteration(0, True, False, False)
            pe.wait_ge(select_made, 1)
            iteration(1, True, True, False)
            with pe.Fori(2, BLOCKS - 1) as b:
                iteration(b, True, True, True)
            iteration(BLOCKS - 1, True, True, True)
            iteration(BLOCKS, False, True, True)
            iteration(BLOCKS + 1, False, False, True)

        @block.scalar
        def _(act):
            def copy(out, in_):
                return act.activation(out, in_, ACT.Copy)

            def hi(b, c):
                act.wait_ge(raw_loaded[c % RING], b * (16 * CH // RING) + 16 * (c // RING + 1))
                if not (isinstance(b, int) and b == 0 and c < RING):
                    act.wait_ge(chunk_used, b * CH + (c - RING + 1))
                n = CHUNKS[c] * width(b)
                copy(adj_hi[:, c % RING, 0:n], raw[:, c % RING, 0:n]).then_inc(hi_ready, 1)

            def h_hi_part(g):
                n = min(4, TILES - 4 * g)
                act.wait_ge(h_full, g + 1)
                copy(h_hi[:, 4 * g:4 * g + n, :].rearrange("p t d -> p (t d)"),
                     pre[:, g % 2, 0:n * D]).then_inc(h_hi_made, 1)

            def normalise(source, i, u, done):
                for q in range(Q):
                    last = act.activation(rows[0:u, q, :], source(q), ACT.Identity,
                                          bias=shift[0:u, i, q:q + 1], scale=rstd[0:u, i, q:q + 1])
                last.then_inc(done, 1)

            def relu_hidden(b, age, k):
                w = width(b - age)
                act.wait_ge(hid_done, upto(b, age, HC, k))
                if before(b, age, k, 2) is not None:
                    act.wait_ge(hid_ready, before(b, age, k, 2))
                act.activation(pre[:, k % 2, 0:w], hid[k % 2][:, 0:w], ACT.Relu,
                               bias=b1[:, k:k + 1]).then_inc(pre_ready, 1)

            def split_hidden(b, age, k):
                w = width(b - age)
                act.wait_ge(hid_ready, upto(b, age, HC, k))
                if before(b, age, k, SR) is not None:
                    act.wait_ge(hid_used, before(b, age, k, SR))
                copy(hid_hi[:, k % SR, 0:w], hid_sb[:, k % HR, 0:w]).then_inc(hid_hi_made, 1)

            def iteration(b, adj, next_adj, prev, old):
                w = width(b)
                wp = width(b - 1)
                for c in range(CH):
                    if isinstance(b, int) and b == 0:
                        for g in range(H_AHEAD, GROUPS):
                            if c == chunk_of(H_MADE[g]):
                                h_hi_part(g)
                    if adj and c == CH - 1:
                        act.wait_ge(chunk_used, upto(b, 0, CH, CH - 1))
                        act.activation(cols[:, 0:w], acc[:, 0:w], ACT.Relu, bias=b_user).then_inc(acc_read, 1)
                    if adj and c + AHEAD_HI < CH:
                        hi(b, c + AHEAD_HI)
                    elif next_adj and c + AHEAD_HI >= CH:
                        hi(b + 1, c + AHEAD_HI - CH)
                    if isinstance(b, int) and b == 1 and c in W_SPLIT:
                        i = W_SPLIT.index(c)
                        act.wait_ge(w_loaded[i], 16)
                        copy((w1_hi, w2_hi)[i // 4][:, quarter(i)], w_raw[i]).then_inc(w_hi_made, 1)
                    if prev and c == chunk_of(TURN_LN) - 1:
                        act.wait_ge(x1_shift, upto(b, 1, 1, 0))
                        normalise(lambda q: turn_a[0:wp // Q, q * D:(q + 1) * D], 0, wp // Q, x1_normed)
                    if prev and c == chunk_of(TURN_LN):
                        act.wait_ge(ln_turned, upto(b, 1, 1, 0))
                        copy(ln_parts(b, 1)[0][:, 0:wp], turn_b[:, 0:wp]).then_inc(ln_hi_made, 1)
                        copy(cols[:, 0:wp], turn_b[:, 0:wp]).then_inc(ln_cols, 1)
                    if prev and c == chunk_of(GATE) + 2:
                        act.wait_ge(gap_ready, upto(b, 1, 1, 0))
                        act.activation(egap[:, :], gap[:, :], ACT.Exp).then_inc(egap_ready, 1)
                    if prev and c == chunk_of(TURN_C):
                        act.wait_ge(comb_turned, upto(b, 1, 1, 0))
                        copy(combT[:, 0:wp], turn_b[0:CR, 0:wp]).then_inc(combT_ready, 1)
                    for age in (1, 2):
                        for k, slot in enumerate(layer1_slots(b, age)):
                            if (prev, old)[age - 1] and FIRST[c] <= slot < FIRST[c + 1]:
                                relu_hidden(b, age, k)
                            if (prev, old)[age - 1] and FIRST[c] <= slot + TO_SPLIT < FIRST[c + 1]:
                                split_hidden(b, age, k)
                    if adj and c == chunk_of(TURN_X) - 3:
                        act.wait_ge(x_shift, upto(b, 0, 1, 0))
                        normalise(lambda q: rows[0:w // Q, q, :], 1, w // Q, x_normed)
                    if adj and c == chunk_of(TURN_X):
                        act.wait_ge(x_turned, upto(b, 0, 1, 0))
                        copy(xln_hi[:, 0:w], turn_a[:, 0:w]).then_inc(xln_hi_made, 1)

            hi(0, 0)
            for g in range(H_AHEAD):
                h_hi_part(g)
            for c in range(1, AHEAD_HI):
                hi(0, c)
            act.wait_ge(select_loaded, 16)
            copy(select[:, :], select_raw).then_inc(select_made, 1)
            act.wait_ge(start_loaded, 16)
            copy(b2_both[:, :], b2_raw).then_inc(small_made, 1)
            act.wait_ge(const_loaded, 16)
            copy(wu_hi[:, :], wuT).then_inc(small_made, 1)
            iteration(0, True, True, False, False)
            iteration(1, True, True, True, False)
            with act.Fori(2, BLOCKS - 2) as b:
                iteration(b, True, True, True, True)
            iteration(BLOCKS - 2, True, True, True, True)
            iteration(BLOCKS - 1, True, False, True, True)
            iteration(BLOCKS, False, False, True, True)
            iteration(BLOCKS + 1, False, False, False, True)

        @block.gpsimd
        def _(pool):
            def root(i, steps, count, rooted):
                pool.wait_ge(steps, count)
                pool.tensor_tensor(rstd[:, i, :], var_eps[:, i, :], minus_half[:, :], ALU.pow).then_inc(rooted, 1)

            def split_hidden(b, age, k):
                w = width(b - age)
                pool.wait_ge(hid_hi_made, upto(b, age, HC, k))
                pool.tensor_tensor(hid_lo[:, k % SR, 0:w], hid_sb[:, k % HR, 0:w], hid_hi[:, k % SR, 0:w],
                                   ALU.subtract).then_inc(hid_lo_made, 1)

            def h_lo_part(g):
                n = min(4, TILES - 1 - 4 * g)
                pool.wait_ge(h_hi_made, g + 1)
                pool.tensor_tensor(h_lo[:, 4 * g:4 * g + n, :].rearrange("p t d -> p (t d)"),
                                   pre[:, g % 2, 0:n * D],
                                   h_hi[:, 4 * g:4 * g + n, :].rearrange("p t d -> p (t d)"),
                                   ALU.subtract).then_inc(h_lo_made, 1)

            def w_lo_part(i):
                pool.wait_ge(w_hi_made, i + 1)
                pool.tensor_tensor((w1_lo, w2_lo)[i // 4][:, quarter(i)], w_raw[i],
                                   (w1_hi, w2_hi)[i // 4][:, quarter(i)], ALU.subtract).then_inc(w_lo_made, 1)

            def iteration(b, adj, prev, old):
                for s in range(TILES):
                    if isinstance(b, int) and b == 0:
                        if s in H_MADE:
                            h_lo_part(H_MADE.index(s))
                    if isinstance(b, int) and b == 1:
                        for i, c in enumerate(W_SPLIT):
                            if s == FIRST[c]:
                                w_lo_part(i)
                    if prev and s == TURN_X1:
                        root(0, x1_stats, upto(b, 1, 3, 2), x1_rstd)
                    for age in (1, 2):
                        for k, slot in enumerate(layer1_slots(b, age)):
                            if (prev, old)[age - 1] and slot + TO_SPLIT == s:
                                split_hidden(b, age, k)
                    if adj and s == TURN_X - 10:
                        root(1, x_stats, upto(b, 0, 3, 2), x_rstd)

            pool.memset(minus_half[:, :], -0.5).then_inc(half_made, 1)
            pool.wait_ge(half_made, 1)
            for g in range(H_AHEAD):
                h_lo_part(g)
            iteration(0, True, False, False)
            iteration(1, True, True, False)
            with pool.Fori(2, BLOCKS - 1) as b:
                iteration(b, True, True, True)
            iteration(BLOCKS - 1, True, True, True)
            iteration(BLOCKS, False, True, True)
            iteration(BLOCKS + 1, False, False, True)

        @block.vector
        def _(dve):
            def lo(b, c):
                dve.wait_ge(hi_ready, upto(b, 0, CH, c))
                if not (isinstance(b, int) and b == 0 and c < LO_RING):
                    dve.wait_ge(chunk_used, b * CH + (c - LO_RING + 1))
                w = width(b)
                n = (CHUNKS[c] - (c == CH - 1)) * w
                if n > 0:
                    last = dve.tensor_tensor(adj_lo[:, c % LO_RING, 0:n], raw[:, c % RING, 0:n],
                                             adj_hi[:, c % RING, 0:n], ALU.subtract)
                if c == CH - 1:
                    low = slice(2 * QUAD, P)
                    last = dve.tensor_tensor(adj_hi[low, c % RING, n:n + w], raw[low, c % RING, n:n + w],
                                             adj_hi[low, c % RING, n:n + w], ALU.subtract)
                last.then_inc(lo_ready, 1)

            def h_with_bias(g):
                n = min(4, TILES - 4 * g) * D
                dve.wait_ge(h_made, g + 1)
                if g == 0:
                    dve.wait_ge(bias_loaded, 16)
                if g >= 2:
                    dve.wait_ge(h_lo_made, g - 1)
                dve.tensor_tensor(pre[:, g % 2, 0:n], hid[g % 2][:, 0:n], item_bc[:, 0:n], ALU.add)\
                   .then_inc(h_full, 1)

            def h_last_tile():
                g = GROUPS - 1
                at = TILES - 1 - 4 * g
                dve.wait_ge(h_hi_made, GROUPS)
                for low in (slice(QUAD, 2 * QUAD), slice(3 * QUAD, P)):
                    last = dve.tensor_tensor(h_hi[low, TILES - 1, :], pre[low, g % 2, at * D:(at + 1) * D],
                                             h_hi[low, TILES - 1, :], ALU.subtract)
                last.then_inc(h_last_made, 1)

            def carry_wait():
                dve.memset(spacer[:, :], 0.0)

            def moments_of(source, i, u, b, age, steps):
                for q in range(Q):
                    last = dve.bn_stats(stats[0:u, i, q, :], source(q))
                last.then_inc(steps, 1)
                dve.wait_ge(steps, upto(b, age, 3, 0))
                carry_wait()
                for q in range(Q):
                    last = dve.bn_aggr(moments[0:u, i, q, :], stats[0:u, i, q, :])
                last.then_inc(steps, 1)
                dve.wait_ge(steps, upto(b, age, 3, 1))
                dve.tensor_scalar(var_eps[0:u, i, :], moments[0:u, i, :, 1], EPS, None, ALU.add).then_inc(steps, 1)

            def shift_of(i, u, b, age, rooted, done):
                dve.wait_ge(rooted, upto(b, age, 1, 0))
                dve.scalar_tensor_tensor(out=shift[0:u, i, :], in0=moments[0:u, i, :, 0], scalar=-1.0,
                                         in1=rstd[0:u, i, :], op0=ALU.mult, op1=ALU.mult).then_inc(done, 1)

            def wide(v):
                return v.broadcast_to([P, Q, E])

            def twice(v):
                return v.unsqueeze(2).broadcast_to([P, Q, 2, E])

            def router_steps(b, age, step):
                def then(instruction):
                    nonlocal step
                    step += 1
                    instruction.then_inc(router, 1)
                    dve.wait_ge(router, upto(b, age, ROUTER_STEPS, step - 1))
                return then

            def route_top(b, age):
                then = router_steps(b, age, 0)
                u = width(b - age) // Q
                dve.wait_ge(gate_done, upto(b, age, 1, 0))
                then(dve.tensor_tensor(logits[0:u, :, :], turn_a[0:u, 0:Q * E].rearrange("p (q e) -> p q e", q=Q),
                                       gate_bias[0:u, :, :], ALU.add))
                carry_wait()
                for q in range(Q):
                    last = dve.max(top[:, q, :], logits[:, q, :])
                then(last)
                dve.tensor_tensor(gap[:, :], top[:, :, 1], top[:, :, 0], ALU.subtract).then_inc(gap_ready, 1)
                for q in range(Q):
                    last = dve.max_index(top_at[:, q, :], top[:, q, :], logits[:, q, :])
                then(last)
                then(dve.tensor_copy(top_f[:, :, :], top_at[:, :, 0:2]))
                for j in range(2):
                    last = dve.tensor_tensor(hot[:, j, :, :], iota, wide(top_f[:, :, j:j + 1]), ALU.is_equal)
                last.then_inc(router, 1)

            def route_weights(b, age):
                then = router_steps(b, age, 5)
                dve.wait_ge(egap_ready, upto(b, age, 1, 0))
                then(dve.tensor_scalar(den[:, :], egap[:, :], 1.0, None, ALU.add))
                then(dve.reciprocal(wt[:, 0, :], den[:, :]))
                then(dve.tensor_tensor(wt[:, 1, :], egap[:, :], wt[:, 0, :], ALU.mult))
                for j in range(2):
                    last = dve.tensor_tensor(hot[:, j, :, :], hot[:, j, :, :],
                                             wide(wt[:, j, :].unsqueeze(2)), ALU.mult)
                then(last)
                then(dve.tensor_tensor(comb[:, :, :], hot[:, 0, :, :], hot[:, 1, :, :], ALU.add))
                then(dve.tensor_copy(comb_hi[:, :, :], comb[:, :, :]))
                hi = twice(comb_hi[:, :, :].bitcast(F32))
                dve.tensor_copy(comb_two[:, :, :, 0:E], hi)
                dve.tensor_tensor(comb_two[:, :, :, E:2 * E], twice(comb[:, :, :]), hi,
                                  ALU.subtract).then_inc(comb_ready, 1)

            def weigh(b, age, k):
                w = width(b - age)
                dve.wait_ge(pre_ready, upto(b, age, HC, k))
                if k == 0:
                    dve.wait_ge(wgt_done, upto(b, age, 1, 0))
                if before(b, age, k, HR) is not None:
                    dve.wait_ge(hid_lo_made, before(b, age, k, HR))
                dve.tensor_tensor(hid_sb[:, k % HR, 0:w], pre[:, k % 2, 0:w], wgt[:, 0:w],
                                  ALU.mult).then_inc(hid_ready, 1)

            def result(b, age):
                w = width(b - age)
                dve.wait_ge(hid_used, upto(b, age, HC, HC - 1))
                dve.wait_ge(old_ready, upto(b, age, 1, 0))
                if not (isinstance(b, int) and b == age):
                    dve.wait_ge(out_stored, upto(b, age + 1, 16, 15))
                dve.tensor_tensor(out_sb[:, 0:w], sum_bank(b, age)[:, 0:w], x1T_old[:, 0:w], ALU.add).then_inc(out_ready, 1)

            def keep_x1(b, age):
                w = width(b - age)
                if not (isinstance(b, int) and b == age):
                    dve.wait_ge(out_ready, upto(b, age + 1, 1, 0))
                dve.wait_ge(x1_ready, upto(b, age, 1, 0))
                dve.tensor_copy(x1T_old[:, 0:w], x1T[:, 0:w]).then_inc(old_ready, 1)

            def iteration(b, adj, next_adj, prev, old):
                w = width(b)
                u = width(b - 1) // Q
                for c in range(CH):
                    if isinstance(b, int) and b == 0:
                        for g in range(H_AHEAD, GROUPS):
                            if c == chunk_of(H_MADE[g]):
                                h_with_bias(g)
                    if adj and c + AHEAD_LO < CH:
                        lo(b, c + AHEAD_LO)
                    elif next_adj and c + AHEAD_LO >= CH:
                        lo(b + 1, c + AHEAD_LO - CH)
                    if isinstance(b, int) and b == 0 and c == chunk_of(H_MADE[-1]):
                        h_last_tile()
                    if prev and c == chunk_of(TURN_X1):
                        dve.wait_ge(x1_turned, upto(b, 1, 1, 0))
                        moments_of(lambda q: turn_a[0:u, q * D:(q + 1) * D], 0, u, b, 1, x1_stats)
                    if prev and c == chunk_of(TURN_X1) + 1:
                        shift_of(0, u, b, 1, x1_rstd, x1_shift)
                    if prev and c == chunk_of(TURN_LN) + 1:
                        dve.wait_ge(ln_cols, upto(b, 1, 1, 0))
                        ln = ln_parts(b, 1)
                        dve.tensor_tensor(ln[1][:, 0:Q * u], cols[:, 0:Q * u], ln[0][:, 0:Q * u], ALU.subtract)\
                           .then_inc(ln_lo_made, 1)
                    if prev and c == chunk_of(GATE) + 1:
                        route_top(b, 1)
                    if prev and c == chunk_of(GATE) + 2:
                        route_weights(b, 1)
                    for age in (1, 2):
                        for k, slot in enumerate(layer1_slots(b, age)):
                            if (prev, old)[age - 1] and FIRST[c] <= slot < FIRST[c + 1]:
                                weigh(b, age, k)
                    if old and c == result_chunk(b) + 1:
                        result(b, 2)
                    if prev and c == result_chunk(b) + 2:
                        keep_x1(b, 1)
                    if adj and c == chunk_of(TURN_X) - 6:
                        dve.wait_ge(x_loaded, upto(b, 0, 16, 15))
                        moments_of(lambda q: rows[0:w // Q, q, :], 1, w // Q, b, 0, x_stats)
                    if adj and c == chunk_of(TURN_X) + 1:
                        dve.wait_ge(xln_hi_made, upto(b, 0, 1, 0))
                        dve.tensor_tensor(xln_lo[:, 0:w], turn_a[:, 0:w], xln_hi[:, 0:w], ALU.subtract)\
                           .then_inc(xln_lo_made, 1)
                    if adj and c == chunk_of(TURN_X) - 5:
                        shift_of(1, w // Q, b, 0, x_rstd, x_shift)
                if adj:
                    dve.wait_ge(acc_read, upto(b, 0, 1, 0))
                    if prev:
                        dve.wait_ge(old_ready, upto(b, 1, 1, 0))
                    dve.wait_ge(xT_loaded, upto(b, 0, 16, 15))
                    dve.tensor_tensor(x1T[:, 0:w], cols[:, 0:w], xT_sb[:, 0:w], ALU.add).then_inc(x1_ready, 1)

            dve.memset(var_eps[:, :, :], 1.0)
            dve.memset(logits[:, :, :], 0.0)
            h_with_bias(0)
            h_with_bias(1)
            lo(0, 0)
            h_with_bias(2)
            for c in range(1, AHEAD_LO):
                lo(0, c)
            dve.wait_ge(start_loaded, 16)
            dve.tensor_tensor(gate_bias[:, :, :], bg, bias, ALU.add).then_inc(small_made, 1)
            dve.wait_ge(small_made, 3)
            dve.tensor_tensor(wu_lo[:, :], wuT, wu_hi[:, :], ALU.subtract).then_inc(small_made, 1)
            dve.scalar_tensor_tensor(out=b2_both[:, :], in0=b2_both[:, :], scalar=b2_sign, in1=b2_low,
                                     op0=ALU.mult, op1=ALU.add).then_inc(small_made, 1)
            iteration(0, True, True, False, False)
            iteration(1, True, True, True, False)
            iteration(2, True, True, True, True)
            with dve.Fori(3, BLOCKS - 2) as b:
                iteration(b, True, True, True, True)
            iteration(BLOCKS - 2, True, True, True, True)
            iteration(BLOCKS - 1, True, False, True, True)
            iteration(BLOCKS, False, False, True, True)
            iteration(BLOCKS + 1, False, False, False, True)


def kernel(**inputs):
    import numpy as np
    import concourse.bacc as bacc
    from concourse.bass_utils import run_bass_kernel_spmd as run

    a = {k: np.asarray(v) for k, v in inputs.items()}
    x, adj = a["x"], a["adj"]
    f32 = np.float32

    def by_block(v, layout):
        full = [layout(v[b * BLOCK:(b + 1) * BLOCK]) for b in range(FULL)]
        return np.stack(full), layout(v[FULL * BLOCK:])

    def items_padded(v):
        t = np.zeros((TILES * P, v.shape[1]), f32)
        t[:N - TAIL] = v[:N - TAIL]
        for row in range(N - TAIL, TILES * P, QUAD):
            t[row:row + TAIL] = v[N - TAIL:]
        return t

    def adj_layout(v):
        t = items_padded(v.T)
        return t.reshape(TILES, P, len(v)).transpose(1, 0, 2).reshape(P, TILES * len(v))

    adj_t, adj_t_last = by_block(adj, adj_layout)
    x_rows, x_rows_last = by_block(x, lambda v: v.reshape(Q, -1, D).transpose(1, 0, 2).reshape(-1, Q * D))
    x_t, x_t_last = by_block(x, lambda v: v.T)
    item_t = items_padded(a["L0_gnn_item_feat"]).T
    consts = np.zeros((P, C_END), f32)
    consts[:, C_ID:C_ID + P] = np.eye(P, dtype=f32)
    consts[:, C_WU:C_WU + D] = a["L0_gnn_W_user"].T
    consts[:, C_WG:C_WG + E] = a["L0_ffn_Wg"]
    consts[:, C_B1:C_B1 + HC] = a["L0_ffn_b1"].reshape(E, HC, PER).transpose(0, 2, 1).reshape(P, HC)
    consts[:, C_BU] = a["L0_gnn_b_user"]
    consts[:, C_IOTA:C_IOTA + Q * E] = np.tile(np.arange(E, dtype=f32), Q)
    start = np.zeros((P, S_END), f32)
    start[:, S_WI:S_WI + D] = a["L0_gnn_W_item"].T
    for row in range(0, CR, E):
        start[row:row + E, S_B2:S_B2 + D] = a["L0_ffn_b2"]
        if row >= 2 * E:
            start[row:row + E, S_B2_LOW:S_B2_LOW + D] = a["L0_ffn_b2"]
    start[0:CR, S_SIGN] = [1.0] * (2 * E) + [-1.0] * (2 * E)
    start[:, S_BG:S_BG + Q * E] = np.tile(a["L0_ffn_bg"], Q)
    start[:, S_BIAS:S_BIAS + Q * E] = np.tile(a["L0_ffn_bias"], Q)
    selector = np.zeros((CR, P), f32)
    for e in range(E):
        selector[[e, E + e], e * PER:(e + 1) * PER] = 1.0
    arrays = {
        "adjT": adj_t,
        "adjT_last": adj_t_last,
        "itemT": item_t,
        "x": x_rows,
        "x_last": x_rows_last,
        "xT": x_t,
        "xT_last": x_t_last,
        "w1": a["L0_ffn_W1"].reshape(E, D, HC, PER).transpose(1, 2, 0, 3).reshape(D, HC * P),
        "w2": a["L0_ffn_W2"].reshape(E, HC, PER, D).transpose(0, 2, 1, 3).reshape(P, HC * D),
        "consts": consts,
        "item_bias": np.tile(a["L0_gnn_b_item"], (P, 4)),
        "selector": selector,
        "start": start,
    }
    nc = bacc.Bacc("TRN2", target_bir_lowering=False, num_devices=1, dynamic_dma_scratch_size=1024)
    feed, args = {}, []
    for name, array in arrays.items():
        feed[name + "_dram"] = np.ascontiguousarray(array)
        args.append(nc.dram_tensor(name + "_dram", array.shape, F32, kind="ExternalInput").ap())
    for name, shape in (("outT_dram", (FULL, D, BLOCK)), ("outT_last_dram", (D, LAST))):
        args.append(nc.dram_tensor(name, shape, F32, kind="ExternalOutput").ap())
    build(nc, *args)
    r = run(nc, [feed], core_ids=[0])
    out_t = r.results[0]["outT_dram"].reshape(FULL, D, BLOCK)
    last_t = r.results[0]["outT_last_dram"].reshape(D, LAST)
    return np.concatenate([out_t.transpose(0, 2, 1).reshape(FULL * BLOCK, D), last_t.T], axis=0)
```
